# Optimizing a Trainium2 kernel written in Bass

```python
import numpy as np
import jax
import jax.numpy as jnp

def _softmax(x, axis=-1):
    return jax.nn.softmax(x, axis=axis)
def _gelu(x):
    return jax.nn.gelu(x, approximate=True)
def _silu(x):
    return jax.nn.silu(x)
def _sigmoid(x):
    return jax.nn.sigmoid(x)
def _layernorm(x, axis=-1, eps=1e-5):
    m = jnp.mean(x, axis=axis, keepdims=True)
    v = jnp.var(x, axis=axis, keepdims=True)
    return (x - m) / jnp.sqrt(v + eps)
def _scatter_add(tgt, idx, src, axis=0):
    return tgt.at[idx].add(src)
def _segment_sum(src, seg, n):
    return jax.ops.segment_sum(src, seg, n)

kernel_name = 'mk_conv_preact_d1_conv_nchw192_ee3bb5'

def setup_inputs(seed: int = 0):
    np.random.seed(seed)
    _w = jnp.asarray
    def _rec_inputs():
        import jax
        import jax.numpy as jnp
        _gk = jax.random.key(seed)
        x = -0.0002221 + 1 * jax.random.normal(jax.random.fold_in(_gk, 1), (8, 192, 128, 128), jnp.float32)
        return x
    x = _rec_inputs()
    def _L0_conv_setup():
        import jax, jax.numpy as jnp
        import numpy as np
        B, C, H, W, D = (8, 192, 128, 128, 64)

        def _gru_scan(seq, W_ih, W_hh, b_ih, b_hh):
            N, T, Dh = (seq.shape[0], seq.shape[1], W_hh.shape[1])
            x_gates = jnp.einsum('ntd,gd->ntg', seq, W_ih) + b_ih
            h0 = jnp.zeros((N, Dh), seq.dtype)

            def step(h, xg):
                hg = h @ W_hh.T + b_hh
                xr, xz, xn = jnp.split(xg, 3, axis=-1)
                hr, hz, hn = jnp.split(hg, 3, axis=-1)
                r = jax.nn.sigmoid(xr + hr)
                z = jax.nn.sigmoid(xz + hz)
                n = jnp.tanh(xn + r * hn)
                h_new = (1.0 - z) * n + z * h
                return (h_new, h_new)
            _, hs = jax.lax.scan(step, h0, jnp.swapaxes(x_gates, 0, 1))
            return jnp.swapaxes(hs, 0, 1)

        def _scan_direction(x, Wi, bi, W_ih, W_hh, b_ih, b_hh, Wo, bo, transpose, reverse):
            b, c, h, w = x.shape
            xs = jnp.transpose(x, (0, 3, 2, 1)) if transpose else jnp.transpose(x, (0, 2, 3, 1))
            if reverse:
                xs = xs[:, :, ::-1, :]
            A, T = (xs.shape[1], xs.shape[2])
            seq = xs.reshape(b * A, T, c) @ Wi.T + bi
            hs = _gru_scan(seq, W_ih, W_hh, b_ih, b_hh)
            out = hs @ Wo.T + bo
            out = out.reshape(b, A, T, c)
            if reverse:
                out = out[:, :, ::-1, :]
            return jnp.transpose(out, (0, 3, 2, 1)) if transpose else jnp.transpose(out, (0, 3, 1, 2))
        key = jax.random.key(seed)
        ks = jax.random.split(key, 9)
        s = 0.1
        return {'x': jax.random.normal(ks[0], (B, C, H, W), jnp.float32), 'Wi': jax.random.normal(ks[1], (D, C), jnp.float32) * s, 'bi': jax.random.normal(ks[2], (D,), jnp.float32) * s, 'W_ih': jax.random.normal(ks[3], (3 * D, D), jnp.float32) * s, 'W_hh': jax.random.normal(ks[4], (3 * D, D), jnp.float32) * s, 'b_ih': jax.random.normal(ks[5], (3 * D,), jnp.float32) * s, 'b_hh': jax.random.normal(ks[6], (3 * D,), jnp.float32) * s, 'Wo': jax.random.normal(ks[7], (C, D), jnp.float32) * s, 'bo': jax.random.normal(ks[8], (C,), jnp.float32) * s}
    _L0_conv_all = _L0_conv_setup()
    _L0_conv_in = {k: v for k, v in _L0_conv_all.items() if k in ('Wi', 'bi', 'W_ih', 'W_hh', 'b_ih', 'b_hh', 'Wo', 'bo', )}
    del _L0_conv_all

    return {
        "x": x,
        "L0_conv_Wi": _L0_conv_in["Wi"],
        "L0_conv_bi": _L0_conv_in["bi"],
        "L0_conv_W_ih": _L0_conv_in["W_ih"],
        "L0_conv_W_hh": _L0_conv_in["W_hh"],
        "L0_conv_b_ih": _L0_conv_in["b_ih"],
        "L0_conv_b_hh": _L0_conv_in["b_hh"],
        "L0_conv_Wo": _L0_conv_in["Wo"],
        "L0_conv_bo": _L0_conv_in["bo"],
    }

def reference(x, L0_conv_Wi, L0_conv_bi, L0_conv_W_ih, L0_conv_W_hh, L0_conv_b_ih, L0_conv_b_hh, L0_conv_Wo, L0_conv_bo):
    import jax
    import jax.numpy as jnp
    def _L0_conv_ref(x, Wi, bi, W_ih, W_hh, b_ih, b_hh, Wo, bo):
        import jax, jax.numpy as jnp
        import numpy as np
        B, C, H, W, D = (8, 192, 128, 128, 64)

        def _gru_scan(seq, W_ih, W_hh, b_ih, b_hh):
            N, T, Dh = (seq.shape[0], seq.shape[1], W_hh.shape[1])
            x_gates = jnp.einsum('ntd,gd->ntg', seq, W_ih) + b_ih
            h0 = jnp.zeros((N, Dh), seq.dtype)

            def step(h, xg):
                hg = h @ W_hh.T + b_hh
                xr, xz, xn = jnp.split(xg, 3, axis=-1)
                hr, hz, hn = jnp.split(hg, 3, axis=-1)
                r = jax.nn.sigmoid(xr + hr)
                z = jax.nn.sigmoid(xz + hz)
                n = jnp.tanh(xn + r * hn)
                h_new = (1.0 - z) * n + z * h
                return (h_new, h_new)
            _, hs = jax.lax.scan(step, h0, jnp.swapaxes(x_gates, 0, 1))
            return jnp.swapaxes(hs, 0, 1)

        def _scan_direction(x, Wi, bi, W_ih, W_hh, b_ih, b_hh, Wo, bo, transpose, reverse):
            b, c, h, w = x.shape
            xs = jnp.transpose(x, (0, 3, 2, 1)) if transpose else jnp.transpose(x, (0, 2, 3, 1))
            if reverse:
                xs = xs[:, :, ::-1, :]
            A, T = (xs.shape[1], xs.shape[2])
            seq = xs.reshape(b * A, T, c) @ Wi.T + bi
            hs = _gru_scan(seq, W_ih, W_hh, b_ih, b_hh)
            out = hs @ Wo.T + bo
            out = out.reshape(b, A, T, c)
            if reverse:
                out = out[:, :, ::-1, :]
            return jnp.transpose(out, (0, 3, 2, 1)) if transpose else jnp.transpose(out, (0, 3, 1, 2))
        p = (Wi, bi, W_ih, W_hh, b_ih, b_hh, Wo, bo)
        right = _scan_direction(x, *p, transpose=False, reverse=False)
        down = _scan_direction(x, *p, transpose=True, reverse=False)
        left = _scan_direction(x, *p, transpose=False, reverse=True)
        up = _scan_direction(x, *p, transpose=True, reverse=True)
        return (right + down + left + up) / 4.0

    def _gn(v, G=32, eps=1e-5):
        B_, C_, H_, W_ = v.shape
        g = v.reshape(B_, G, C_ // G, H_, W_)
        m = jnp.mean(g, axis=(2, 3, 4), keepdims=True)
        s = jnp.var(g, axis=(2, 3, 4), keepdims=True)
        return ((g - m) / jnp.sqrt(s + eps)).reshape(v.shape)

    def _ln_c(v, eps=1e-6):
        m = jnp.mean(v, axis=1, keepdims=True)
        s = jnp.var(v, axis=1, keepdims=True)
        return (v - m) / jnp.sqrt(s + eps)

    def _ln_t(v, eps=1e-5):
        m = jnp.mean(v, axis=-1, keepdims=True)
        s = jnp.var(v, axis=-1, keepdims=True)
        return (v - m) / jnp.sqrt(s + eps)

    def _to_tokens(v):
        B_, C_, H_, W_ = v.shape
        return v.reshape(B_, C_, H_ * W_).transpose(0, 2, 1)
    def _from_tokens(t, like):
        B_, C_, H_, W_ = like.shape
        return t.transpose(0, 2, 1).reshape(B_, C_, H_, W_)

    x = x + _L0_conv_ref(_gn(x), L0_conv_Wi, L0_conv_bi, L0_conv_W_ih, L0_conv_W_hh, L0_conv_b_ih, L0_conv_b_hh, L0_conv_Wo, L0_conv_bo)
    return x


_drawn_inputs = setup_inputs


def setup_inputs(seed=0):
    import zlib

    import numpy as np

    out = dict(_drawn_inputs(seed))
    spreads = {}
    factors = {}
    for name, (base, spread) in spreads.items():
        noise = np.random.default_rng([zlib.crc32(name.encode()), seed]).standard_normal(out[name].shape)
        drawn = base * np.exp(spread * noise) if base else spread * noise
        out[name] = jnp.asarray(drawn.astype(out[name].dtype))
    for name, factor in factors.items():
        out[name] = (out[name] * factor).astype(out[name].dtype)
    return out
```

```python
import concourse.bass as bass
from concourse import mybir
from contextlib import ExitStack


def gru_scan_2d_kernel(nc: bass.Bass, x, wi_t, bi, w_ih_t, w_hh_t, b_ih, b_hh, wo_t, bo,
                       avg_part, sel_low, sel_high_a, sel_high_b, out):
    fp32 = mybir.dt.float32
    ALU = mybir.AluOpType
    ACT = mybir.ActivationFunctionType

    B, C, HH, WW = x.shape
    D = wi_t.shape[1]
    P = 128
    GROUPS = 32
    EPS = 1e-5
    PX = HH * WW
    PAIRS = B // 2
    T = WW
    N = HH
    N2 = 2 * N
    TILE = 512
    TILES = PX // TILE
    XSLOTS = 4
    OSLOTS = 2
    CLOW = P
    CHIGH = C - CLOW
    SPART = C * PX // P
    CHUNK = 768
    CPI = SPART // CHUNK
    BNF = CHUNK // 2
    NSTAT = 2 * CPI
    UN = 4
    N_WEIGHT_LOADS = 6 + 2 * (5 + 3 * 4)
    assert CPI * UN == T and CHIGH == D == 64 and HH == WW == P

    x_px = x.rearrange("b c h w -> b c (h w)")
    out_px = out.rearrange("b c h w -> b c (h w)")
    x_flat = x.rearrange("b c h w -> b (c h w)").rearrange("b (p m) -> b p m", p=P)

    ctx = ExitStack()
    with ctx:
        def sb(name, shape, dt=fp32):
            return ctx.enter_context(nc.sbuf_tensor(name, shape, dt))

        def sem(name):
            return ctx.enter_context(nc.semaphore(name))

        seq = sb("seq", [P, PX])
        hsum = sb("hsum", [P, PX])
        xt = sb("xt", [P, XSLOTS, 3, TILE])
        ot = sb("ot", [P, OSLOTS, 3, TILE])
        sx = sb("sx", [P, 2, CHUNK])
        bn = sb("bn", [P, 2, NSTAT * 6])
        h = sb("h", [P, 2, 2, N2])
        r = sb("r", [P, 2, N2])
        z = sb("z", [P, 2, N2])
        t1 = sb("t1", [P, 2, N2])
        t2 = sb("t2", [P, 2, N2])
        n = sb("n", [P, 2, N2])
        d = sb("d", [P, 2, N2])
        e = sb("e", [P, 2, N2])
        wi_low = sb("wi_low", [P, D])
        wi_high = sb("wi_high", [P, P])
        wa = sb("wa", [P, D])
        wb = sb("wb", [P, D])
        wc = sb("wc", [P, P])
        wx = sb("wx", [P, 3, P])
        wh = sb("wh", [P, 3, P])
        wo_a = sb("wo_a", [P, P])
        wo_b = sb("wo_b", [P, P])
        wo_c = sb("wo_c", [P, P])
        s_avg = sb("s_avg", [P, P])
        s_low = sb("s_low", [P, P])
        s_ha = sb("s_ha", [P, P])
        s_hb = sb("s_hb", [P, P])
        bih = sb("bih", [P, 3])
        bhh = sb("bhh", [P, 3])
        brz = sb("brz", [P, 2])
        bi2 = sb("bi2", [P, 1])
        bo_low = sb("bo_low", [P, 1])
        bo_high = sb("bo_high", [P, 1])
        mv = sb("mv", [P, 2, 2])
        sm = sb("sm", [P, 12, 3])
        bseq = sb("bseq", [P, 1])
        spare = sb("spare", [P, 16])

        bank = [ctx.enter_context(nc.psum_tensor(f"bank{i}", [P, TILE], fp32)) for i in range(8)]
        rx_ps = [bank[0], bank[3]]
        hn_ps = [bank[1], bank[4]]
        z_ps = [bank[2], bank[5]]
        fin_ps = [bank[0:3], bank[3:6]]
        proj_ps = bank[6:8]
        stat_ps = bank[6]

        w_loaded = sem("w_loaded")
        w_zeroed = sem("w_zeroed")
        w_ready = sem("w_ready")
        x_loaded = [sem(f"x_loaded{i}") for i in range(XSLOTS)]
        x_finished = sem("x_finished")
        out_stored = [sem(f"out_stored{i}") for i in range(OSLOTS)]
        sx_loaded = [sem(f"sx_loaded{i}") for i in range(2)]
        sx_used = [sem(f"sx_used{i}") for i in range(2)]
        stat_dve = sem("stat_dve")
        stat_pe = sem("stat_pe")
        stat_sd = sem("stat_sd")
        seq_ready = sem("seq_ready")
        proj_ready = sem("proj_ready")
        fin_ready = sem("fin_ready")
        pre_r = [sem(f"pre_r{c}") for c in range(2)]
        pre_n = [sem(f"pre_n{c}") for c in range(2)]
        pre_z = [sem(f"pre_z{c}") for c in range(2)]
        r_ready = [sem(f"r_ready{c}") for c in range(2)]
        z_ready = [sem(f"z_ready{c}") for c in range(2)]
        t1_ready = [sem(f"t1_ready{c}") for c in range(2)]
        t2_ready = [sem(f"t2_ready{c}") for c in range(2)]
        n_ready = [sem(f"n_ready{c}") for c in range(2)]
        d_ready = [sem(f"d_ready{c}") for c in range(2)]
        e_ready = [sem(f"e_ready{c}") for c in range(2)]
        h_ready = [sem(f"h_ready{c}") for c in range(2)]
        h_added = [sem(f"h_added{c}") for c in range(2)]
        hsum_zeroed = sem("hsum_zeroed")

        H1 = T + 1
        NSD = 17
        NSP = 3

        seq_hw = seq[:, :].rearrange("p (h w) -> p h w", w=WW)
        hsum_hw = hsum[:, :].rearrange("p (h w) -> p h w", w=WW)

        def pixels(view, c, back, t):
            s = (T - 1) - t if back else t
            if c == 0:
                return view[:, :, bass.ds(s, 1)].rearrange("p h w -> p (h w)")
            return view[:, bass.ds(s, 1), :].rearrange("p h w -> p (h w)")

        block = ctx.enter_context(nc.Block())

        @block.sync
        def _(sp):
            loads = [(wi_low[:, :], wi_t[0:CLOW, :]), (s_avg[:, :], avg_part), (s_low[:, :], sel_low),
                     (s_ha[:, :], sel_high_a), (s_hb[:, :], sel_high_b)]
            bo_col = bo.rearrange("(c o) -> c o", o=1)
            bi_col = bi.rearrange("(c o) -> c o", o=1)
            loads.append((bo_low[:, :], bo_col[0:CLOW, :]))
            sp.wait_ge(w_zeroed, 1)
            for k in range(2):
                half = slice(k * D, (k + 1) * D)
                loads += [(wi_high[half, half], wi_t[CLOW:C, :]),
                          (wo_c[half, half], wo_t[:, CLOW:C]),
                          ((wo_a, wo_b)[k][half, :], wo_t[:, 0:CLOW]),
                          (bi2[half, :], bi_col),
                          (bo_high[half, :], bo_col[CLOW:C, :])]
                for g in range(3):
                    loads += [(wx[half, g, half], w_ih_t[:, g * D:(g + 1) * D]),
                              (wh[half, g, half], w_hh_t[:, g * D:(g + 1) * D]),
                              (bih[half, g:g + 1], b_ih.rearrange("(c o) -> c o", o=1)[g * D:(g + 1) * D, :]),
                              (bhh[half, g:g + 1], b_hh.rearrange("(c o) -> c o", o=1)[g * D:(g + 1) * D, :])]
            assert len(loads) == N_WEIGHT_LOADS
            for dst, src in loads:
                sp.dma_start(dst, src).then_inc(w_loaded, 16)

            def load_stats(pair):
                with sp.Fori(0, CPI) as i:
                    for a in range(2):
                        sp.wait_ge(sx_used[a], 1 + CPI * pair + i)
                        src = x_flat[bass.ds(2 * pair + a, 1), :, bass.ds(i * CHUNK, CHUNK)]
                        sp.dma_start(sx[:, a, :], src.rearrange("b p m -> (b p) m")).then_inc(sx_loaded[a], 16)

            def load_x(pair, i, s):
                img = 2 * pair
                px = bass.ds((i + s) * TILE, TILE)

                def src(k, lo, hi):
                    return x_px[bass.ds(img + k, 1), lo:hi, px].rearrange("b c n -> (b c) n")
                sp.dma_start(xt[:, s, 0, :], src(0, 0, CLOW)).then_inc(x_loaded[s], 16)
                sp.dma_start(xt[:, s, 1, :], src(1, 0, CLOW)).then_inc(x_loaded[s], 16)
                sp.dma_start(xt[0:D, s, 2, :], src(0, CLOW, C)).then_inc(x_loaded[s], 16)
                sp.dma_start(xt[D:P, s, 2, :], src(1, CLOW, C)).then_inc(x_loaded[s], 16)

            def pair_loads(g, stats):
                for s in range(XSLOTS):
                    sp.wait_ge(x_finished, TILES * g + s + 1)
                    load_x(g, 0, s)
                with sp.Fori(1, TILES // XSLOTS) as j:
                    i = j * XSLOTS
                    for s in range(XSLOTS):
                        sp.wait_ge(proj_ready, TILES * g + i + s - XSLOTS + 1)
                        load_x(g, i, s)
                if stats:
                    load_stats(g + 1)
                for s in range(XSLOTS):
                    sp.wait_ge(proj_ready, TILES * g + TILES - XSLOTS + s + 1)
                    load_x(g, 0, s)
                with sp.Fori(1, TILES // XSLOTS) as j:
                    i = j * XSLOTS
                    for s in range(XSLOTS):
                        sp.wait_ge(x_finished, TILES * g + i + s + 1)
                        load_x(g, i, s)

            load_stats(0)
            with sp.Fori(0, PAIRS - 1) as g:
                pair_loads(g, True)
            pair_loads(PAIRS - 1, False)

        @block.gpsimd
        def _(pool):
            for w in (wi_high, wo_a, wo_b, wo_c, wx):
                pool.memset(w[:], 0.0)
            pool.memset(wh[:], 0.0).then_inc(w_zeroed, 1)
            with pool.Fori(0, PAIRS) as g:
                with pool.Fori(0, T // 2) as j:
                    t0 = j * 2
                    pool.wait_ge(hsum_zeroed, g + 1)
                    for u in range(2):
                        for c in range(2):
                            pool.wait_ge(h_ready[c], H1 * g + t0 + u + 2)
                            pool.wait_ge(h_added[1 - c], 1 + T * g + t0 + u + c)
                            for back in range(2):
                                px = pixels(hsum_hw, c, back, t0 + u)
                                ins = pool.tensor_tensor(px, px, h[:, c, (u + 1) % 2, back * N:(back + 1) * N],
                                                         ALU.add)
                            ins.then_inc(h_added[c], 1)

        @block.scalar
        def _(act):
            with act.Fori(0, PAIRS) as g:
                act.wait_ge(stat_dve, NSD * g + 6)
                act.activation(sm[:, 1, :], sm[:, 0, :], ACT.Sqrt).then_inc(stat_sd, 1)
                act.wait_ge(stat_dve, NSD * g + NSD)
                with act.Fori(0, TILES // 2) as j:
                    i = j * 2
                    for s in range(2):
                        act.wait_ge(proj_ready, TILES * g + i + s + 1)
                        act.activation(seq[:, bass.ds((i + s) * TILE, TILE)], proj_ps[s][:, :], ACT.Identity,
                                       bias=bseq[:, 0:1]).then_inc(seq_ready, 1)
                with act.Fori(0, T) as t:
                    for c in range(2):
                        act.wait_ge(pre_r[c], T * g + t + 1)
                        act.activation(r[:, c, :], rx_ps[c][:, 0:N2], ACT.Sigmoid, bias=brz[:, 0:1])\
                           .then_inc(r_ready[c], 1)
                        act.wait_ge(pre_z[c], T * g + t + 1)
                        act.activation(z[:, c, :], z_ps[c][:, 0:N2], ACT.Sigmoid, bias=brz[:, 1:2])\
                           .then_inc(z_ready[c], 1)
                        act.wait_ge(t2_ready[c], 1 + T * g + t + 1)
                        act.activation(n[:, c, :], t2[:, c, :], ACT.Tanh, bias=bih[:, 2:3])\
                           .then_inc(n_ready[c], 1)

                def store(i, s):
                    act.wait_ge(x_finished, XSLOTS + TILES * g + i + s + 1)
                    px = bass.ds((i + s) * TILE, TILE)

                    def dst(k, lo, hi):
                        return out_px[bass.ds(2 * g + k, 1), lo:hi, px].rearrange("b c n -> (b c) n")
                    act.dma_start(dst(0, 0, CLOW), ot[:, s, 0, :]).then_inc(out_stored[s], 16)
                    act.dma_start(dst(1, 0, CLOW), ot[:, s, 1, :]).then_inc(out_stored[s], 16)
                    act.dma_start(dst(0, CLOW, C), ot[0:D, s, 2, :]).then_inc(out_stored[s], 16)
                    act.dma_start(dst(1, CLOW, C), ot[D:P, s, 2, :]).then_inc(out_stored[s], 16)
                with act.Fori(0, TILES // OSLOTS) as j:
                    i = j * OSLOTS
                    for s in range(OSLOTS):
                        store(i, s)
            for s in range(OSLOTS):
                act.wait_ge(out_stored[s], 64 * (PAIRS * TILES // OSLOTS + 1))

        @block.tensor
        def _(pe):
            pe.wait_ge(w_loaded, 16 * N_WEIGHT_LOADS)
            pe.wait_ge(w_ready, 4)
            with pe.Fori(0, PAIRS) as g:
                pe.wait_ge(stat_dve, NSD * g + 2)
                pe.matmul(stat_ps[:, 0:2], s_avg[:, :], mv[:, :, 0], start=True, stop=True).then_inc(stat_pe, 1)
                pe.wait_ge(stat_dve, NSD * g + 5)
                pe.matmul(stat_ps[:, 8:10], s_low[:, :], mv[:, 0, :], start=True, stop=True)
                pe.matmul(stat_ps[:, 10:12], s_low[:, :], mv[:, 1, :], start=True, stop=True)
                pe.matmul(stat_ps[:, 12:14], s_ha[:, :], mv[:, 0, :], start=True, stop=False)
                pe.matmul(stat_ps[:, 12:14], s_hb[:, :], mv[:, 1, :], start=False, stop=True).then_inc(stat_pe, 1)
                pe.wait_ge(stat_dve, NSD * g + 13)
                pe.matmul(stat_ps[:, 16:17], wi_high[:, :], sm[:, 8, 2:3], start=True, stop=False,
                          skip_group_check=True)
                pe.matmul(stat_ps[0:D, 16:17], wi_low[:, :], sm[:, 8, 0:1], start=False, stop=True,
                          skip_group_check=True)
                pe.matmul(stat_ps[D:P, 16:17], wi_low[:, :], sm[:, 8, 1:2], start=False, stop=True,
                          skip_group_check=True).then_inc(stat_pe, 1)
                with pe.Fori(0, TILES // XSLOTS) as j:
                    i = j * XSLOTS
                    pe.wait_ge(stat_dve, NSD * g + NSD)
                    pe.wait_ge(x_finished, XSLOTS + TILES * g)
                    for s in range(XSLOTS):
                        pe.wait_ge(x_loaded[s], 64 * (2 * (TILES // XSLOTS) * g + 1) + 16 * i)
                        pe.wait_ge(seq_ready, TILES * g + i + s + 1)
                        ps = proj_ps[s % 2]
                        pe.matmul(ps[:, :], wc[:, :], xt[:, s, 2, :], start=True, stop=False, skip_group_check=True)
                        pe.matmul(ps[0:D, :], wa[:, :], xt[:, s, 0, :], start=False, stop=True,
                                  skip_group_check=True)
                        pe.matmul(ps[D:P, :], wb[:, :], xt[:, s, 1, :], start=False, stop=True,
                                  skip_group_check=True).then_inc(proj_ready, 1)
                with pe.Fori(0, T // 2) as j:
                    t0 = j * 2
                    pe.wait_ge(seq_ready, 2 + TILES * (g + 1))
                    for u in range(2):
                        t = t0 + u
                        for c in range(2):
                            rx, hn, zz = rx_ps[c], hn_ps[c], z_ps[c]

                            def x_part(ps, col, gate, start):
                                for back in range(2):
                                    pe.matmul(ps[:, col + back * N:col + (back + 1) * N], wx[:, gate, :],
                                              pixels(seq_hw, c, back, t), start=start and back == 0, stop=False,
                                              skip_group_check=True)
                            pe.wait_ge(z_ready[c], 1 + T * g + t)
                            x_part(zz, 0, 1, True)
                            pe.wait_ge(t2_ready[c], 1 + T * g + t)
                            x_part(rx, 0, 0, True)
                            x_part(rx, N2, 2, False)
                            pe.wait_ge(h_ready[c], H1 * g + t + 1)
                            hc = h[:, c, u, :]
                            pe.matmul(rx[:, 0:N2], wh[:, 0, :], hc, start=False, stop=True,
                                      skip_group_check=True).then_inc(pre_r[c], 1)
                            pe.matmul(hn[:, 0:N2], wh[:, 2, :], hc, start=True, stop=True,
                                      skip_group_check=True).then_inc(pre_n[c], 1)
                            pe.matmul(zz[:, 0:N2], wh[:, 1, :], hc, start=False, stop=True,
                                      skip_group_check=True).then_inc(pre_z[c], 1)
                with pe.Fori(0, TILES // 2) as j:
                    i = j * 2
                    for c in range(2):
                        pe.wait_ge(h_added[c], 1 + T * (g + 1))
                    for s in range(2):
                        pe.wait_ge(x_finished, XSLOTS - 1 + TILES * g + i + s)
                        hs = hsum[:, bass.ds((i + s) * TILE, TILE)]
                        pe.matmul(fin_ps[s][0][:, :], wo_a[:, :], hs, start=True, stop=True)
                        pe.matmul(fin_ps[s][1][:, :], wo_b[:, :], hs, start=True, stop=True)
                        pe.matmul(fin_ps[s][2][:, :], wo_c[:, :], hs, start=True, stop=True).then_inc(fin_ready, 1)

        @block.vector
        def _(dve):
            tokens = [(x_finished, XSLOTS), (seq_ready, 2), (fin_ready, 1)] + [(o, 64) for o in out_stored]
            for c in range(2):
                tokens += [(s, 1) for s in (h_added[c], z_ready[c], t2_ready[c], sx_used[c])]
            for k, (token, count) in enumerate(tokens):
                dve.memset(spare[:, k:k + 1], 0.0).then_inc(token, count)
            dve.wait_ge(w_loaded, 16 * N_WEIGHT_LOADS)
            dve.tensor_tensor(brz[:, :], bih[:, 0:2], bhh[:, 0:2], ALU.add).then_inc(w_ready, 1)
            dve.tensor_scalar(wo_a[:, :], wo_a[:, :], 0.25, None, ALU.mult).then_inc(w_ready, 1)
            dve.tensor_scalar(wo_b[:, :], wo_b[:, :], 0.25, None, ALU.mult).then_inc(w_ready, 1)
            dve.tensor_scalar(wo_c[:, :], wo_c[:, :], 0.25, None, ALU.mult).then_inc(w_ready, 1)

            def chunk_stats(pair, i, a):
                dve.wait_ge(sx_loaded[a], 16 * (CPI * pair + i + 1))
                for k in range(2):
                    ins = dve.bn_stats(bn[:, a, :].rearrange("p (s k) -> p s k", k=12)[:, bass.ds(i, 1), 6 * k:6 * k + 6]
                                       .rearrange("p s k -> p (s k)"), sx[:, a, k * BNF:(k + 1) * BNF])
                ins.then_inc(sx_used[a], 1)

            def scan(g, stats):
                with dve.Fori(0, T // UN) as i:
                    for u in range(UN):
                        t = UN * i + u
                        for c in range(2):
                            old, new = h[:, c, u % 2, :], h[:, c, (u + 1) % 2, :]
                            k = T * g + t + 1
                            dve.wait_ge(pre_n[c], k)
                            dve.wait_ge(r_ready[c], k)
                            dve.scalar_tensor_tensor(out=t1[:, c, :], in0=hn_ps[c][:, 0:N2],
                                                     scalar=bhh[:, 2:3], in1=r[:, c, :], op0=ALU.add,
                                                     op1=ALU.mult).then_inc(t1_ready[c], 1)
                            dve.wait_ge(t1_ready[c], k)
                            dve.tensor_tensor(t2[:, c, :], rx_ps[c][:, N2:2 * N2], t1[:, c, :], ALU.add)\
                               .then_inc(t2_ready[c], 1)
                            if stats and u == 1:
                                chunk_stats(g + 1, i, c)
                            dve.wait_ge(n_ready[c], k)
                            dve.tensor_tensor(d[:, c, :], old, n[:, c, :], ALU.subtract).then_inc(d_ready[c], 1)
                            dve.wait_ge(z_ready[c], k + 1)
                            dve.wait_ge(d_ready[c], k)
                            dve.tensor_tensor(e[:, c, :], z[:, c, :], d[:, c, :], ALU.mult).then_inc(e_ready[c], 1)
                            dve.wait_ge(e_ready[c], k)
                            dve.wait_ge(h_added[c], T * g + t)
                            dve.tensor_tensor(new, n[:, c, :], e[:, c, :], ALU.add).then_inc(h_ready[c], 1)

            def stat_chain(g):
                base = NSD * g

                def done(k):
                    dve.wait_ge(stat_dve, base + k)
                for c in range(2):
                    dve.wait_ge(h_added[c], 1 + T * g)
                    dve.wait_ge(sx_used[c], 1 + CPI * (g + 1))
                    dve.memset(h[:, c, 0, :], 0.0).then_inc(h_ready[c], 1)
                for a in range(2):
                    dve.bn_aggr(mv[:, a, :], bn[:, a, :]).then_inc(stat_dve, 1)
                done(2)
                dve.wait_ge(stat_pe, NSP * g + 1)
                dve.tensor_tensor(sm[:, 2, 0:2], mv[:, :, 0], stat_ps[:, 0:2], ALU.subtract).then_inc(stat_dve, 1)
                done(3)
                dve.tensor_tensor(sm[:, 3, 0:2], sm[:, 2, 0:2], sm[:, 2, 0:2], ALU.mult).then_inc(stat_dve, 1)
                done(4)
                dve.tensor_tensor(mv[:, :, 1], mv[:, :, 1], sm[:, 3, 0:2], ALU.add).then_inc(stat_dve, 1)
                dve.wait_ge(stat_pe, NSP * g + 2)
                chan = stat_ps[:, 8:14].rearrange("p (i k) -> p i k", k=2)
                dve.tensor_scalar(sm[:, 0, :], chan[:, :, 1], EPS, None, ALU.add).then_inc(stat_dve, 1)
                dve.tensor_copy(sm[:, 4, :], chan[:, :, 0]).then_inc(stat_dve, 1)
                dve.wait_ge(stat_sd, g + 1)
                dve.reciprocal(sm[:, 5, :], sm[:, 1, :]).then_inc(stat_dve, 1)
                done(8)
                dve.tensor_tensor(sm[:, 6, :], sm[:, 5, :], sm[:, 5, :], ALU.mult).then_inc(stat_dve, 1)
                done(9)
                dve.tensor_tensor(sm[:, 7, :], sm[:, 6, :], sm[:, 0, :], ALU.mult).then_inc(stat_dve, 1)
                done(10)
                dve.tensor_scalar(sm[:, 10, :], sm[:, 7, :], -0.5, 1.5, ALU.mult, ALU.add).then_inc(stat_dve, 1)
                done(11)
                dve.tensor_tensor(sm[:, 11, :], sm[:, 5, :], sm[:, 10, :], ALU.mult).then_inc(stat_dve, 1)
                done(12)
                dve.scalar_tensor_tensor(out=sm[:, 8, :], in0=sm[:, 4, :], scalar=-1.0, in1=sm[:, 11, :],
                                         op0=ALU.mult, op1=ALU.mult).then_inc(stat_dve, 1)
                dve.tensor_scalar(wa[:, :], wi_low[:, :], sm[:, 11, 0:1], None, ALU.mult).then_inc(stat_dve, 1)
                dve.tensor_scalar(wb[:, :], wi_low[:, :], sm[:, 11, 1:2], None, ALU.mult).then_inc(stat_dve, 1)
                dve.tensor_scalar(wc[:, :], wi_high[:, :], sm[:, 11, 2:3], None, ALU.mult).then_inc(stat_dve, 1)
                dve.wait_ge(stat_pe, NSP * g + 3)
                dve.tensor_tensor(bseq[:, :], stat_ps[:, 16:17], bi2[:, :], ALU.add).then_inc(stat_dve, 1)
                dve.wait_ge(fin_ready, 1 + TILES * g)
                dve.memset(hsum[:, :], 0.0).then_inc(hsum_zeroed, 1)

            def finish(g):
                with dve.Fori(0, TILES // XSLOTS) as j:
                    i = j * XSLOTS
                    for s in range(XSLOTS):
                        o = s % OSLOTS
                        dve.wait_ge(x_loaded[s], 64 * ((2 * g + 1) * (TILES // XSLOTS) + 1) + 16 * i)
                        if s < OSLOTS:
                            dve.wait_ge(out_stored[o], 64 * ((TILES // OSLOTS) * g + 1) + 32 * i)
                        else:
                            dve.wait_ge(out_stored[o], 64 * ((TILES // OSLOTS) * g + 2) + 32 * i)
                        dve.wait_ge(fin_ready, 1 + TILES * g + i + s + 1)
                        for k in range(3):
                            ins = dve.scalar_tensor_tensor(
                                out=ot[:, o, k, :], in0=fin_ps[s % 2][k][:, :],
                                scalar=(bo_low if k < 2 else bo_high)[:, 0:1], in1=xt[:, s, k, :],
                                op0=ALU.add, op1=ALU.add)
                        ins.then_inc(x_finished, 1)

            with dve.Fori(0, CPI) as i:
                for a in range(2):
                    chunk_stats(0, i, a)
            with dve.Fori(0, PAIRS - 1) as g:
                stat_chain(g)
                scan(g, True)
                finish(g)
            stat_chain(PAIRS - 1)
            scan(PAIRS - 1, False)
            finish(PAIRS - 1)


def kernel(x, L0_conv_Wi, L0_conv_bi, L0_conv_W_ih, L0_conv_W_hh, L0_conv_b_ih, L0_conv_b_hh, L0_conv_Wo, L0_conv_bo):
    import numpy as np
    import concourse.bacc as bacc
    from concourse.bass_utils import run_bass_kernel_spmd

    part = np.arange(128) // 4
    chan = np.arange(192) // 6
    share = np.float32(0.25)
    avg_part = (part[:, None] == part[None, :]).astype(np.float32) * share
    sel = (part[:, None] == chan[None, :]).astype(np.float32) * share
    sel_high_a = np.zeros((128, 128), np.float32)
    sel_high_b = np.zeros((128, 128), np.float32)
    sel_high_a[:, 0:64] = sel[:, 128:192]
    sel_high_b[:, 64:128] = sel[:, 128:192]

    arrays = {
        "x": np.ascontiguousarray(x),
        "wi_t": np.ascontiguousarray(np.asarray(L0_conv_Wi).T),
        "bi": np.ascontiguousarray(L0_conv_bi),
        "w_ih_t": np.ascontiguousarray(np.asarray(L0_conv_W_ih).T),
        "w_hh_t": np.ascontiguousarray(np.asarray(L0_conv_W_hh).T),
        "b_ih": np.ascontiguousarray(L0_conv_b_ih),
        "b_hh": np.ascontiguousarray(L0_conv_b_hh),
        "wo_t": np.ascontiguousarray(np.asarray(L0_conv_Wo).T),
        "bo": np.ascontiguousarray(L0_conv_bo),
        "avg_part": avg_part,
        "sel_low": np.ascontiguousarray(sel[:, 0:128]),
        "sel_high_a": sel_high_a,
        "sel_high_b": sel_high_b,
    }
    nc = bacc.Bacc("TRN2", target_bir_lowering=False, num_devices=1)
    args = [nc.dram_tensor(name, a.shape, mybir.dt.from_np(a.dtype), kind="ExternalInput").ap()
            for name, a in arrays.items()]
    out = nc.dram_tensor("out", arrays["x"].shape, mybir.dt.float32, kind="ExternalOutput").ap()
    gru_scan_2d_kernel(nc, *args, out)
    return run_bass_kernel_spmd(nc, [arrays], core_ids=[0]).results[0]["out"]
```

```python
import concourse.bass as bass
from concourse import mybir
from contextlib import ExitStack


def gru_scan_2d_kernel(nc: bass.Bass, x, wi_t, bi, w_ih_t, w_hh_t, b_ih, b_hh, wo_t, bo,
                       avg_part, sel_low, sel_high_a, sel_high_b, out):
    fp32 = mybir.dt.float32
    fp16 = mybir.dt.float16
    ALU = mybir.AluOpType
    ACT = mybir.ActivationFunctionType

    B, C, HH, WW = x.shape
    D = wi_t.shape[1]
    P = 128
    GROUPS = 32
    EPS = 1e-5
    PX = HH * WW
    PAIRS = B // 2
    T = WW
    N = HH
    N2 = 2 * N
    TILE = 512
    TILES = PX // TILE
    XSLOTS = 4
    OSLOTS = 2
    CLOW = P
    CHIGH = C - CLOW
    SPART = C * PX // P
    CHUNK = 768
    CPI = SPART // CHUNK
    BNF = CHUNK // 2
    NSTAT = 2 * CPI
    UN = 4
    PRO = SPART // (3 * TILE)
    N_WEIGHT_LOADS = 6 + 2 * (5 + 3 * 4)
    assert CPI * UN == T and CHIGH == D == 64 and HH == WW == P

    x_px = x.rearrange("b c h w -> b c (h w)")
    out_px = out.rearrange("b c h w -> b c (h w)")
    x_flat = x.rearrange("b c h w -> b (c h w)").rearrange("b (p m) -> b p m", p=P)

    ctx = ExitStack()
    with ctx:
        def sb(name, shape, dt=fp32):
            return ctx.enter_context(nc.sbuf_tensor(name, shape, dt))

        def sem(name):
            return ctx.enter_context(nc.semaphore(name))

        seq_hi = sb("seq_hi", [P, PX], fp16)
        seq_lo = sb("seq_lo", [P, PX], fp16)
        hsum = sb("hsum", [P, PX])
        xt = sb("xt", [P, XSLOTS, 3, TILE])
        ot = sb("ot", [P, OSLOTS, 3, TILE])
        sx = sb("sx", [P, 2, CHUNK])
        bn = sb("bn", [P, 2, NSTAT * 6])
        h = sb("h", [P, 2, 2, N2])
        r = sb("r", [P, 2, N2])
        z = sb("z", [P, 2, N2])
        t1 = sb("t1", [P, 2, N2])
        t2 = sb("t2", [P, 2, N2])
        n = sb("n", [P, 2, N2])
        w = sb("w", [P, 2, N2])
        v = sb("v", [P, 2, N2])
        u_n = t1
        h_hi = sb("h_hi", [P, 2, N2], fp16)
        h_lo = sb("h_lo", [P, 2, N2], fp16)
        wi_low = sb("wi_low", [P, D])
        wi_high = sb("wi_high", [P, P])
        wa = sb("wa", [P, D])
        wb = sb("wb", [P, D])
        wc = sb("wc", [P, P])
        w_parts = sb("w_parts", [P, 4, 3, P], fp16)
        wx_hi, wx_lo, wh_hi, wh_lo = (w_parts[:, k] for k in range(4))
        w_gru = hsum[:, 0:2 * 3 * P].rearrange("p (k g m) -> p k g m", k=2, g=3)
        wx, wh = w_gru[:, 0], w_gru[:, 1]
        wo_a = sb("wo_a", [P, P])
        wo_b = sb("wo_b", [P, P])
        wo_c = sb("wo_c", [P, P])
        s_avg = sb("s_avg", [P, P])
        s_low = sb("s_low", [P, P])
        s_ha = sb("s_ha", [P, P])
        s_hb = sb("s_hb", [P, P])
        bih = sb("bih", [P, 3])
        bhh = sb("bhh", [P, 3])
        brz = sb("brz", [P, 3])
        bi2 = sb("bi2", [P, 1])
        bo_low = sb("bo_low", [P, 1])
        bo_high = sb("bo_high", [P, 1])
        mv = sb("mv", [P, 2, 2])
        sm = sb("sm", [P, 12, 3])
        bseq = sb("bseq", [P, 1])
        zeros = sb("zeros", [P, TILE])
        spare = sb("spare", [P, 32])

        bank = [ctx.enter_context(nc.psum_tensor(f"bank{i}", [P, TILE], fp32)) for i in range(8)]
        rx_ps = [bank[0], bank[3]]
        hn_ps = [bank[1], bank[4]]
        z_ps = [bank[2], bank[5]]
        fin_ps = [bank[0:3], bank[3:6]]
        proj_ps = bank[6:8]
        stat_ps = bank[6]

        w_loaded = sem("w_loaded")
        w_zeroed = sem("w_zeroed")
        w_ready = sem("w_ready")
        x_loaded = [sem(f"x_loaded{i}") for i in range(XSLOTS)]
        x_finished = sem("x_finished")
        out_stored = [sem(f"out_stored{i}") for i in range(OSLOTS)]
        sx_loaded = [sem(f"sx_loaded{i}") for i in range(2)]
        sx_used = [sem(f"sx_used{i}") for i in range(2)]
        stat_dve = sem("stat_dve")
        stat_pe = sem("stat_pe")
        stat_sd = sem("stat_sd")
        seq_ready = sem("seq_ready")
        proj_ready = sem("proj_ready")
        fin_ready = sem("fin_ready")
        pre_r = [sem(f"pre_r{c}") for c in range(2)]
        pre_n = [sem(f"pre_n{c}") for c in range(2)]
        pre_z = [sem(f"pre_z{c}") for c in range(2)]
        r_ready = [sem(f"r_ready{c}") for c in range(2)]
        z_ready = [sem(f"z_ready{c}") for c in range(2)]
        t1_ready = [sem(f"t1_ready{c}") for c in range(2)]
        t2_ready = [sem(f"t2_ready{c}") for c in range(2)]
        n_ready = [sem(f"n_ready{c}") for c in range(2)]
        w_gate_ready = [sem(f"w_gate_ready{c}") for c in range(2)]
        v_ready = [sem(f"v_ready{c}") for c in range(2)]
        u_ready = [sem(f"u_ready{c}") for c in range(2)]
        h_ready = [sem(f"h_ready{c}") for c in range(2)]
        hi_ready = [sem(f"hi_ready{c}") for c in range(2)]
        lo_ready = [sem(f"lo_ready{c}") for c in range(2)]
        SPLITS = [T + 1, T]
        hi_seq_ready = sem("hi_seq_ready")
        pro_loaded = [sem(f"pro_loaded{i}") for i in range(XSLOTS)]
        pro_used = [sem(f"pro_used{i}") for i in range(XSLOTS)]
        h_added = [sem(f"h_added{c}") for c in range(2)]
        hsum_zeroed = sem("hsum_zeroed")

        H1 = T + 1
        NSD = 17
        NSP = 3

        seq_hi_hw = seq_hi[:, :].rearrange("p (h w) -> p h w", w=WW)
        seq_lo_hw = seq_lo[:, :].rearrange("p (h w) -> p h w", w=WW)
        hsum_hw = hsum[:, :].rearrange("p (h w) -> p h w", w=WW)

        def pixels(view, c, back, t):
            s = (T - 1) - t if back else t
            if c == 0:
                return view[:, :, bass.ds(s, 1)].rearrange("p h w -> p (h w)")
            return view[:, bass.ds(s, 1), :].rearrange("p h w -> p (h w)")

        block = ctx.enter_context(nc.Block())

        @block.sync
        def _(sp):
            loads = [(wi_low[:, :], wi_t[0:CLOW, :]), (s_avg[:, :], avg_part), (s_low[:, :], sel_low),
                     (s_ha[:, :], sel_high_a), (s_hb[:, :], sel_high_b)]
            bo_col = bo.rearrange("(c o) -> c o", o=1)
            bi_col = bi.rearrange("(c o) -> c o", o=1)
            loads.append((bo_low[:, :], bo_col[0:CLOW, :]))
            sp.wait_ge(w_zeroed, 1)
            for k in range(2):
                half = slice(k * D, (k + 1) * D)
                loads += [(wi_high[half, half], wi_t[CLOW:C, :]),
                          (wo_c[half, half], wo_t[:, CLOW:C]),
                          ((wo_a, wo_b)[k][half, :], wo_t[:, 0:CLOW]),
                          (bi2[half, :], bi_col),
                          (bo_high[half, :], bo_col[CLOW:C, :])]
                for g in range(3):
                    loads += [(wx[half, g, half], w_ih_t[:, g * D:(g + 1) * D]),
                              (wh[half, g, half], w_hh_t[:, g * D:(g + 1) * D]),
                              (bih[half, g:g + 1], b_ih.rearrange("(c o) -> c o", o=1)[g * D:(g + 1) * D, :]),
                              (bhh[half, g:g + 1], b_hh.rearrange("(c o) -> c o", o=1)[g * D:(g + 1) * D, :])]
            assert len(loads) == N_WEIGHT_LOADS
            for dst, src in loads:
                sp.dma_start(dst, src).then_inc(w_loaded, 16)

            def load_stats(pair):
                with sp.Fori(0, CPI) as i:
                    for a in range(2):
                        sp.wait_ge(sx_used[a], 1 + CPI * (pair - 1) + i)
                        src = x_flat[bass.ds(2 * pair + a, 1), :, bass.ds(i * CHUNK, CHUNK)]
                        sp.dma_start(sx[:, a, :], src.rearrange("b p m -> (b p) m")).then_inc(sx_loaded[a], 16)

            def load_x(pair, i, s):
                img = 2 * pair
                px = bass.ds((i + s) * TILE, TILE)

                def src(k, lo, hi):
                    return x_px[bass.ds(img + k, 1), lo:hi, px].rearrange("b c n -> (b c) n")
                sp.dma_start(xt[:, s, 0, :], src(0, 0, CLOW)).then_inc(x_loaded[s], 16)
                sp.dma_start(xt[:, s, 1, :], src(1, 0, CLOW)).then_inc(x_loaded[s], 16)
                sp.dma_start(xt[0:D, s, 2, :], src(0, CLOW, C)).then_inc(x_loaded[s], 16)
                sp.dma_start(xt[D:P, s, 2, :], src(1, CLOW, C)).then_inc(x_loaded[s], 16)

            def pair_loads(g, stats):
                for s in range(XSLOTS):
                    sp.wait_ge(x_finished, TILES * g + s + 1)
                    load_x(g, 0, s)
                with sp.Fori(1, TILES // XSLOTS) as j:
                    i = j * XSLOTS
                    for s in range(XSLOTS):
                        sp.wait_ge(proj_ready, TILES * g + i + s - XSLOTS + 1)
                        load_x(g, i, s)
                if stats:
                    load_stats(g + 1)
                for s in range(XSLOTS):
                    sp.wait_ge(proj_ready, TILES * g + TILES - XSLOTS + s + 1)
                    load_x(g, 0, s)
                with sp.Fori(1, TILES // XSLOTS) as j:
                    i = j * XSLOTS
                    for s in range(XSLOTS):
                        sp.wait_ge(x_finished, TILES * g + i + s + 1)
                        load_x(g, i, s)

            with sp.Fori(0, PRO // 2) as j:
                for s in range(XSLOTS):
                    sp.wait_ge(pro_used[s], 1 + j)
                    src = x_flat[s // 2:s // 2 + 1, :, bass.ds((2 * j + s % 2) * 3 * TILE, 3 * TILE)]
                    sp.dma_start(xt[:, s, :, :].rearrange("p k n -> p (k n)"), src.rearrange("b p m -> (b p) m"))\
                      .then_inc(pro_loaded[s], 16)
            for s in range(XSLOTS):
                sp.wait_ge(pro_used[s], 1 + PRO // 2)
            with sp.Fori(0, PAIRS - 1) as g:
                pair_loads(g, True)
            pair_loads(PAIRS - 1, False)

        @block.gpsimd
        def _(pool):
            for weight in (wi_high, wo_a, wo_b, wo_c):
                pool.memset(weight[:], 0.0)
            pool.memset(w_gru, 0.0).then_inc(w_zeroed, 1)

            def make_v(g, t, u, c):
                pool.wait_ge(z_ready[c], 1 + T * g + t + 1)
                pool.wait_ge(h_ready[c], H1 * g + t + 1)
                pool.tensor_tensor(v[:, c, :], z[:, c, :], h[:, c, u, :], ALU.mult).then_inc(v_ready[c], 1)

            def add_h(g, t, u, c):
                pool.wait_ge(h_ready[c], H1 * g + t + 2)
                pool.wait_ge(h_added[1 - c], 1 + T * g + t + c)
                for back in range(2):
                    px = pixels(hsum_hw, c, back, t)
                    ins = pool.tensor_tensor(px, px, h[:, c, (u + 1) % 2, back * N:(back + 1) * N], ALU.add)
                ins.then_inc(h_added[c], 1)

            def step(g, t, u, first=False):
                make_v(g, t, u, 0)
                if not first:
                    add_h(g, t - 1, (u + 1) % 2, 1)
                make_v(g, t, u, 1)
                add_h(g, t, u, 0)

            with pool.Fori(0, PAIRS) as g:
                make_v(g, 0, 0, 0)
                make_v(g, 0, 0, 1)
                pool.wait_ge(hsum_zeroed, TILES * (g + 1))
                add_h(g, 0, 0, 0)
                step(g, 1, 1)
                with pool.Fori(1, T // 2) as j:
                    for u in range(2):
                        step(g, 2 * j + u, u)
                add_h(g, T - 1, 1, 1)

        @block.scalar
        def _(act):
            with act.Fori(0, PAIRS) as g:
                act.wait_ge(stat_dve, NSD * g + 6)
                act.activation(sm[:, 1, :], sm[:, 0, :], ACT.Sqrt).then_inc(stat_sd, 1)
                act.preload_act_table(ACT.Sigmoid)
                act.wait_ge(stat_dve, NSD * g + NSD)
                with act.Fori(0, TILES // 2) as j:
                    for s in range(2):
                        act.wait_ge(proj_ready, TILES * g + 2 * j + s + 1)
                        act.activation(seq_hi[:, bass.ds((2 * j + s) * TILE, TILE)], proj_ps[s][:, :], ACT.Identity,
                                       bias=bseq[:, 0:1]).then_inc(hi_seq_ready, 1)

                def split_h(t, u, c):
                    act.wait_ge(h_ready[c], H1 * g + t + 2)
                    act.activation(h_hi[:, c, :], h[:, c, (u + 1) % 2, :], ACT.Copy).then_inc(hi_ready[c], 1)

                def step(t, u, first=False):
                    for c in range(2):
                        act.wait_ge(pre_r[c], T * g + t + 1)
                        act.activation(r[:, c, :], rx_ps[c][:, 0:N2], ACT.Sigmoid, bias=brz[:, 0:1])\
                           .then_inc(r_ready[c], 1)
                        act.wait_ge(pre_z[c], T * g + t + 1)
                        act.activation(z[:, c, :], z_ps[c][:, 0:N2], ACT.Sigmoid, bias=brz[:, 1:2])\
                           .then_inc(z_ready[c], 1)
                        if c == 1:
                            split_h(t, u, 0)
                        elif not first:
                            split_h(t - 1, (u + 1) % 2, 1)
                        act.activation(w[:, c, :], z_ps[c][:, 0:N2], ACT.Sigmoid, bias=brz[:, 2:3], scale=-1.0)\
                           .then_inc(w_gate_ready[c], 1)
                        act.wait_ge(t2_ready[c], 1 + T * g + t + 1)
                        act.activation(n[:, c, :], t2[:, c, :], ACT.Tanh, bias=bih[:, 2:3])\
                           .then_inc(n_ready[c], 1)

                step(0, 0, first=True)
                step(1, 1)
                with act.Fori(1, T // 2) as j:
                    for u in range(2):
                        step(2 * j + u, u)

                def store(i, s):
                    act.wait_ge(x_finished, XSLOTS + TILES * g + i + s + 1)
                    px = bass.ds((i + s) * TILE, TILE)

                    def dst(k, lo, hi):
                        return out_px[bass.ds(2 * g + k, 1), lo:hi, px].rearrange("b c n -> (b c) n")
                    act.dma_start(dst(0, 0, CLOW), ot[:, s, 0, :]).then_inc(out_stored[s], 16)
                    act.dma_start(dst(1, 0, CLOW), ot[:, s, 1, :]).then_inc(out_stored[s], 16)
                    act.dma_start(dst(0, CLOW, C), ot[0:D, s, 2, :]).then_inc(out_stored[s], 16)
                    act.dma_start(dst(1, CLOW, C), ot[D:P, s, 2, :]).then_inc(out_stored[s], 16)
                with act.Fori(0, TILES // OSLOTS) as j:
                    i = j * OSLOTS
                    for s in range(OSLOTS):
                        store(i, s)
            for s in range(OSLOTS):
                act.wait_ge(out_stored[s], 64 * (PAIRS * TILES // OSLOTS + 1))

        @block.tensor
        def _(pe):
            pe.wait_ge(w_loaded, 16 * N_WEIGHT_LOADS)
            pe.wait_ge(w_ready, 10)
            with pe.Fori(0, PAIRS) as g:
                pe.wait_ge(stat_dve, NSD * g + 2)
                pe.matmul(stat_ps[:, 0:2], s_avg[:, :], mv[:, :, 0], start=True, stop=True).then_inc(stat_pe, 1)
                pe.wait_ge(stat_dve, NSD * g + 5)
                pe.matmul(stat_ps[:, 8:10], s_low[:, :], mv[:, 0, :], start=True, stop=True)
                pe.matmul(stat_ps[:, 10:12], s_low[:, :], mv[:, 1, :], start=True, stop=True)
                pe.matmul(stat_ps[:, 12:14], s_ha[:, :], mv[:, 0, :], start=True, stop=False)
                pe.matmul(stat_ps[:, 12:14], s_hb[:, :], mv[:, 1, :], start=False, stop=True).then_inc(stat_pe, 1)
                pe.wait_ge(stat_dve, NSD * g + 13)
                pe.matmul(stat_ps[:, 16:17], wi_high[:, :], sm[:, 8, 2:3], start=True, stop=False,
                          skip_group_check=True)
                pe.matmul(stat_ps[0:D, 16:17], wi_low[:, :], sm[:, 8, 0:1], start=False, stop=True,
                          skip_group_check=True)
                pe.matmul(stat_ps[D:P, 16:17], wi_low[:, :], sm[:, 8, 1:2], start=False, stop=True,
                          skip_group_check=True).then_inc(stat_pe, 1)
                with pe.Fori(0, TILES // XSLOTS) as j:
                    i = j * XSLOTS
                    pe.wait_ge(stat_dve, NSD * g + NSD)
                    pe.wait_ge(x_finished, XSLOTS + TILES * g)
                    for s in range(XSLOTS):
                        pe.wait_ge(x_loaded[s], 64 * (2 * (TILES // XSLOTS) * g + 1) + 16 * i)
                        pe.wait_ge(seq_ready, TILES * g + i + s + 1)
                        ps = proj_ps[s % 2]
                        pe.matmul(ps[:, :], wc[:, :], xt[:, s, 2, :], start=True, stop=False, skip_group_check=True)
                        pe.matmul(ps[0:D, :], wa[:, :], xt[:, s, 0, :], start=False, stop=True,
                                  skip_group_check=True)
                        pe.matmul(ps[D:P, :], wb[:, :], xt[:, s, 1, :], start=False, stop=True,
                                  skip_group_check=True).then_inc(proj_ready, 1)
                with pe.Fori(0, T // 2) as j:
                    t0 = j * 2
                    pe.wait_ge(seq_ready, 2 + TILES * (g + 1))
                    for u in range(2):
                        t = t0 + u
                        for c in range(2):
                            rx, hn, zz = rx_ps[c], hn_ps[c], z_ps[c]

                            def x_part(ps, col, gate, start):
                                for k, (wt, parts) in enumerate(((wx_hi, (seq_hi_hw, seq_lo_hw)), (wx_lo, (seq_hi_hw,)))):
                                    for view in parts:
                                        for back in range(2):
                                            pe.matmul(ps[:, col + back * N:col + (back + 1) * N], wt[:, gate, :],
                                                      pixels(view, c, back, t), stop=False, skip_group_check=True,
                                                      start=start and k == 0 and view is seq_hi_hw and back == 0)
                            pe.wait_ge(w_gate_ready[c], 1 + T * g + t)
                            x_part(zz, 0, 1, True)
                            pe.wait_ge(t2_ready[c], 1 + T * g + t)
                            x_part(rx, 0, 0, True)
                            x_part(rx, N2, 2, False)
                            h_sets = ((rx, 0, pre_r, False), (hn, 2, pre_n, True), (zz, 1, pre_z, False))
                            pe.wait_ge(hi_ready[c], SPLITS[c] * g + t + 1)
                            for ps, gate, _, start in h_sets:
                                for wt in (wh_lo, wh_hi):
                                    pe.matmul(ps[:, 0:N2], wt[:, gate, :], h_hi[:, c, :], stop=False,
                                              start=start and wt is wh_lo, skip_group_check=True)
                            pe.wait_ge(lo_ready[c], SPLITS[c] * g + t + 1)
                            for ps, gate, ready, _ in h_sets:
                                pe.matmul(ps[:, 0:N2], wh_hi[:, gate, :], h_lo[:, c, :], start=False, stop=True,
                                          skip_group_check=True).then_inc(ready[c], 1)
                with pe.Fori(0, TILES // 2) as j:
                    i = j * 2
                    for c in range(2):
                        pe.wait_ge(h_added[c], 1 + T * (g + 1))
                    for s in range(2):
                        pe.wait_ge(x_finished, XSLOTS - 1 + TILES * g + i + s)
                        hs = hsum[:, bass.ds((i + s) * TILE, TILE)]
                        pe.matmul(fin_ps[s][0][:, :], wo_a[:, :], hs, start=True, stop=True)
                        pe.matmul(fin_ps[s][1][:, :], wo_b[:, :], hs, start=True, stop=True)
                        pe.matmul(fin_ps[s][2][:, :], wo_c[:, :], hs, start=True, stop=True).then_inc(fin_ready, 1)

        @block.vector
        def _(dve):
            tokens = [(x_finished, XSLOTS), (seq_ready, 2), (fin_ready, 1)] + [(o, 64) for o in out_stored]
            for c in range(2):
                tokens += [(s, 1) for s in (h_added[c], z_ready[c], w_gate_ready[c], t2_ready[c], sx_used[c])]
            tokens += [(s, 1) for s in pro_used]
            for k, (token, count) in enumerate(tokens):
                dve.memset(spare[:, k:k + 1], 0.0).then_inc(token, count)
            dve.memset(zeros[:, :], 0.0).then_inc(w_ready, 1)
            dve.wait_ge(w_loaded, 16 * N_WEIGHT_LOADS)
            dve.tensor_tensor(brz[:, 0:2], bih[:, 0:2], bhh[:, 0:2], ALU.add).then_inc(w_ready, 1)
            dve.tensor_scalar(wo_a[:, :], wo_a[:, :], 0.25, None, ALU.mult).then_inc(w_ready, 1)
            dve.tensor_scalar(wo_b[:, :], wo_b[:, :], 0.25, None, ALU.mult).then_inc(w_ready, 1)
            dve.tensor_scalar(wo_c[:, :], wo_c[:, :], 0.25, None, ALU.mult).then_inc(w_ready, 1)
            dve.tensor_copy(wx_hi, wx).then_inc(w_ready, 1)
            dve.tensor_copy(wh_hi, wh).then_inc(w_ready, 1)
            dve.wait_ge(w_ready, 7)
            dve.tensor_tensor(wx_lo, wx, wx_hi, ALU.subtract).then_inc(w_ready, 1)
            dve.tensor_tensor(wh_lo, wh, wh_hi, ALU.subtract).then_inc(w_ready, 1)
            dve.tensor_scalar(brz[:, 2:3], brz[:, 1:2], -1.0, None, ALU.mult).then_inc(w_ready, 1)

            def chunk_stats(pair, i, a):
                dve.wait_ge(sx_loaded[a], 16 * (CPI * (pair - 1) + i + 1))
                for k in range(2):
                    ins = dve.bn_stats(bn[:, a, :].rearrange("p (s k) -> p s k", k=12)[:, bass.ds(i, 1), 6 * k:6 * k + 6]
                                       .rearrange("p s k -> p (s k)"), sx[:, a, k * BNF:(k + 1) * BNF])
                ins.then_inc(sx_used[a], 1)

            def scan(g, stats):
                def split_h(t, u, c):
                    dve.wait_ge(hi_ready[c], SPLITS[c] * g + t + 2)
                    dve.tensor_tensor(h_lo[:, c, :], h[:, c, (u + 1) % 2, :], h_hi[:, c, :], ALU.subtract)\
                       .then_inc(lo_ready[c], 1)

                def step(i, t, u, first=False):
                    for c in range(2):
                        k = T * g + t + 1
                        dve.wait_ge(pre_n[c], k)
                        dve.wait_ge(r_ready[c], k)
                        dve.scalar_tensor_tensor(out=t1[:, c, :], in0=hn_ps[c][:, 0:N2], scalar=bhh[:, 2:3],
                                                 in1=r[:, c, :], op0=ALU.add, op1=ALU.mult).then_inc(t1_ready[c], 1)
                        dve.wait_ge(t1_ready[c], k)
                        dve.tensor_tensor(t2[:, c, :], rx_ps[c][:, N2:2 * N2], t1[:, c, :], ALU.add)\
                           .then_inc(t2_ready[c], 1)
                        if c == 1:
                            split_h(t, u % 2, 0)
                        elif not first:
                            split_h(t - 1, (u + 1) % 2, 1)
                        if stats and u == 1:
                            chunk_stats(g + 1, i, c)
                        dve.wait_ge(n_ready[c], k)
                        dve.wait_ge(w_gate_ready[c], k + 1)
                        dve.wait_ge(t2_ready[c], k + 1)
                        dve.tensor_tensor(u_n[:, c, :], w[:, c, :], n[:, c, :], ALU.mult).then_inc(u_ready[c], 1)
                        dve.wait_ge(u_ready[c], k)
                        dve.wait_ge(v_ready[c], k)
                        dve.wait_ge(h_added[c], T * g + t)
                        dve.tensor_tensor(h[:, c, (u + 1) % 2, :], u_n[:, c, :], v[:, c, :], ALU.add)\
                           .then_inc(h_ready[c], 1)

                for t in range(UN):
                    step(0, t, t, first=t == 0)
                with dve.Fori(1, T // UN) as i:
                    for u in range(UN):
                        step(i, UN * i + u, u)

            def stat_chain(g):
                base = NSD * g

                def done(k):
                    dve.wait_ge(stat_dve, base + k)
                for c in range(2):
                    dve.wait_ge(h_added[c], 1 + T * g)
                    dve.wait_ge(sx_used[c], 1 + CPI * g)
                    dve.memset(h[:, c, 0, :], 0.0).then_inc(h_ready[c], 1)
                    dve.memset(h_hi[:, c, :], 0.0).then_inc(hi_ready[c], 1)
                    dve.memset(h_lo[:, c, :], 0.0).then_inc(lo_ready[c], 1)
                for a in range(2):
                    dve.bn_aggr(mv[:, a, :], bn[:, a, :]).then_inc(stat_dve, 1)
                done(2)
                dve.wait_ge(stat_pe, NSP * g + 1)
                dve.tensor_tensor(sm[:, 2, 0:2], mv[:, :, 0], stat_ps[:, 0:2], ALU.subtract).then_inc(stat_dve, 1)
                done(3)
                dve.tensor_tensor(sm[:, 3, 0:2], sm[:, 2, 0:2], sm[:, 2, 0:2], ALU.mult).then_inc(stat_dve, 1)
                done(4)
                dve.tensor_tensor(mv[:, :, 1], mv[:, :, 1], sm[:, 3, 0:2], ALU.add).then_inc(stat_dve, 1)
                dve.wait_ge(stat_pe, NSP * g + 2)
                chan = stat_ps[:, 8:14].rearrange("p (i k) -> p i k", k=2)
                dve.tensor_scalar(sm[:, 0, :], chan[:, :, 1], EPS, None, ALU.add).then_inc(stat_dve, 1)
                dve.tensor_copy(sm[:, 4, :], chan[:, :, 0]).then_inc(stat_dve, 1)
                dve.wait_ge(stat_sd, g + 1)
                dve.reciprocal(sm[:, 5, :], sm[:, 1, :]).then_inc(stat_dve, 1)
                done(8)
                dve.tensor_tensor(sm[:, 6, :], sm[:, 5, :], sm[:, 5, :], ALU.mult).then_inc(stat_dve, 1)
                done(9)
                dve.tensor_tensor(sm[:, 7, :], sm[:, 6, :], sm[:, 0, :], ALU.mult).then_inc(stat_dve, 1)
                done(10)
                dve.tensor_scalar(sm[:, 10, :], sm[:, 7, :], -0.5, 1.5, ALU.mult, ALU.add).then_inc(stat_dve, 1)
                done(11)
                dve.tensor_tensor(sm[:, 11, :], sm[:, 5, :], sm[:, 10, :], ALU.mult).then_inc(stat_dve, 1)
                done(12)
                dve.scalar_tensor_tensor(out=sm[:, 8, :], in0=sm[:, 4, :], scalar=-1.0, in1=sm[:, 11, :],
                                         op0=ALU.mult, op1=ALU.mult).then_inc(stat_dve, 1)
                dve.tensor_scalar(wa[:, :], wi_low[:, :], sm[:, 11, 0:1], None, ALU.mult).then_inc(stat_dve, 1)
                dve.tensor_scalar(wb[:, :], wi_low[:, :], sm[:, 11, 1:2], None, ALU.mult).then_inc(stat_dve, 1)
                dve.tensor_scalar(wc[:, :], wi_high[:, :], sm[:, 11, 2:3], None, ALU.mult).then_inc(stat_dve, 1)
                dve.wait_ge(stat_pe, NSP * g + 3)
                dve.tensor_tensor(bseq[:, :], stat_ps[:, 16:17], bi2[:, :], ALU.add).then_inc(stat_dve, 1)

            def project(g):
                with dve.Fori(0, TILES // 2) as j:
                    for s in range(2):
                        dve.wait_ge(hi_seq_ready, TILES * g + 2 * j + s + 1)
                        px = bass.ds((2 * j + s) * TILE, TILE)
                        dve.scalar_tensor_tensor(out=seq_lo[:, px], in0=proj_ps[s][:, :], scalar=bseq[:, 0:1],
                                                 in1=seq_hi[:, px], op0=ALU.add, op1=ALU.subtract)\
                           .then_inc(seq_ready, 1)
                        dve.wait_ge(fin_ready, 1 + TILES * g)
                        dve.tensor_copy(hsum[:, px], zeros[:, :]).then_inc(hsum_zeroed, 1)

            def finish(g):
                with dve.Fori(0, TILES // XSLOTS) as j:
                    i = j * XSLOTS
                    for s in range(XSLOTS):
                        o = s % OSLOTS
                        dve.wait_ge(x_loaded[s], 64 * ((2 * g + 1) * (TILES // XSLOTS) + 1) + 16 * i)
                        if s < OSLOTS:
                            dve.wait_ge(out_stored[o], 64 * ((TILES // OSLOTS) * g + 1) + 32 * i)
                        else:
                            dve.wait_ge(out_stored[o], 64 * ((TILES // OSLOTS) * g + 2) + 32 * i)
                        dve.wait_ge(fin_ready, 1 + TILES * g + i + s + 1)
                        for k in range(3):
                            ins = dve.scalar_tensor_tensor(
                                out=ot[:, o, k, :], in0=fin_ps[s % 2][k][:, :],
                                scalar=(bo_low if k < 2 else bo_high)[:, 0:1], in1=xt[:, s, k, :],
                                op0=ALU.add, op1=ALU.add)
                        ins.then_inc(x_finished, 1)

            with dve.Fori(0, PRO // 2) as j:
                for s in range(XSLOTS):
                    dve.wait_ge(pro_loaded[s], 16 * (j + 1))
                    flat = xt[:, s, :, :].rearrange("p k n -> p (k n)")
                    per = 3 * TILE // BNF
                    for k in range(per):
                        ins = dve.bn_stats(bn[:, s // 2, bass.ds((2 * j + s % 2) * 6 * per + 6 * k, 6)],
                                           flat[:, k * BNF:(k + 1) * BNF])
                    ins.then_inc(pro_used[s], 1)
            for s in range(XSLOTS):
                dve.wait_ge(pro_used[s], 1 + PRO // 2)
            with dve.Fori(0, PAIRS - 1) as g:
                stat_chain(g)
                project(g)
                scan(g, True)
                finish(g)
            stat_chain(PAIRS - 1)
            project(PAIRS - 1)
            scan(PAIRS - 1, False)
            finish(PAIRS - 1)


def kernel(x, L0_conv_Wi, L0_conv_bi, L0_conv_W_ih, L0_conv_W_hh, L0_conv_b_ih, L0_conv_b_hh, L0_conv_Wo, L0_conv_bo):
    import numpy as np
    import concourse.bacc as bacc
    from concourse.bass_utils import run_bass_kernel_spmd

    part = np.arange(128) // 4
    chan = np.arange(192) // 6
    share = np.float32(0.25)
    avg_part = (part[:, None] == part[None, :]).astype(np.float32) * share
    sel = (part[:, None] == chan[None, :]).astype(np.float32) * share
    sel_high_a = np.zeros((128, 128), np.float32)
    sel_high_b = np.zeros((128, 128), np.float32)
    sel_high_a[:, 0:64] = sel[:, 128:192]
    sel_high_b[:, 64:128] = sel[:, 128:192]

    arrays = {
        "x": np.ascontiguousarray(x),
        "wi_t": np.ascontiguousarray(np.asarray(L0_conv_Wi).T),
        "bi": np.ascontiguousarray(L0_conv_bi),
        "w_ih_t": np.ascontiguousarray(np.asarray(L0_conv_W_ih).T),
        "w_hh_t": np.ascontiguousarray(np.asarray(L0_conv_W_hh).T),
        "b_ih": np.ascontiguousarray(L0_conv_b_ih),
        "b_hh": np.ascontiguousarray(L0_conv_b_hh),
        "wo_t": np.ascontiguousarray(np.asarray(L0_conv_Wo).T),
        "bo": np.ascontiguousarray(L0_conv_bo),
        "avg_part": avg_part,
        "sel_low": np.ascontiguousarray(sel[:, 0:128]),
        "sel_high_a": sel_high_a,
        "sel_high_b": sel_high_b,
    }
    nc = bacc.Bacc("TRN2", target_bir_lowering=False, num_devices=1)
    args = [nc.dram_tensor(name, a.shape, mybir.dt.from_np(a.dtype), kind="ExternalInput").ap()
            for name, a in arrays.items()]
    out = nc.dram_tensor("out", arrays["x"].shape, mybir.dt.float32, kind="ExternalOutput").ap()
    gru_scan_2d_kernel(nc, *args, out)
    return run_bass_kernel_spmd(nc, [arrays], core_ids=[0]).results[0]["out"]
```

```python
import concourse.bass as bass
from concourse import mybir
from contextlib import ExitStack


def gru_scan_2d_kernel(nc: bass.Bass, x, wi_t, bi, w_ih_t, w_hh_t, b_ih, b_hh, wo_t, bo,
                       avg_part, sel_low, sel_high_a, sel_high_b, out):
    fp32 = mybir.dt.float32
    fp16 = mybir.dt.float16
    ALU = mybir.AluOpType
    ACT = mybir.ActivationFunctionType

    B, C, HH, WW = x.shape
    D = wi_t.shape[1]
    P = 128
    EPS = 1e-5
    PX = HH * WW
    PAIRS = B // 2
    T = WW
    N = HH
    N2 = 2 * N
    TILE = 512
    TILES = PX // TILE
    XSLOTS = 8
    ROUNDS = TILES // XSLOTS
    PSLOTS = 4
    CLOW = P
    CHIGH = C - CLOW
    SPART = C * PX // P
    CHUNK = 768
    CPI = SPART // CHUNK
    BNF = CHUNK // 2
    NSTAT = 2 * CPI
    UN = 4
    PRO = SPART // (3 * TILE)
    N_WEIGHT_LOADS = 6 + 2 * (5 + 3 * 4)
    assert CPI * UN == T and CHIGH == D == 64 and HH == WW == P

    x_px = x.rearrange("b c h w -> b c (h w)")
    out_px = out.rearrange("b c h w -> b c (h w)")
    x_flat = x.rearrange("b c h w -> b (c h w)").rearrange("b (p m) -> b p m", p=P)

    ctx = ExitStack()
    with ctx:
        def sb(name, shape, dt=fp32):
            return ctx.enter_context(nc.sbuf_tensor(name, shape, dt))

        def sem(name):
            return ctx.enter_context(nc.semaphore(name))

        seq_hi = sb("seq_hi", [P, PX], fp16)
        seq_lo = sb("seq_lo", [P, PX], fp16)
        hsum = sb("hsum", [P, PX])
        xt = sb("xt", [P, XSLOTS, 3, TILE])
        sx = sb("sx", [P, 2, CHUNK])
        bn = sb("bn", [P, 2, NSTAT * 6])
        h = sb("h", [P, 2, N2])
        r = sb("r", [P, 2, N2])
        z = sb("z", [P, 2, N2])
        t1 = sb("t1", [P, 2, N2])
        t2 = sb("t2", [P, 2, N2])
        v = sb("v", [P, 2, N2])
        n = t2
        u_n = t1
        wi_low = sb("wi_low", [P, D])
        wi_high = sb("wi_high", [P, P])
        wa = sb("wa", [P, D])
        wb = sb("wb", [P, D])
        wc = sb("wc", [P, P])
        wh = sb("wh", [P, 3, P])
        wx_hi = sb("wx_hi", [P, 3, P], fp16)
        wx_lo = sb("wx_lo", [P, 3, P], fp16)
        wx = hsum[:, 0:3 * P].rearrange("p (g m) -> p g m", g=3)
        wo_a = sb("wo_a", [P, P])
        wo_b = sb("wo_b", [P, P])
        wo_c = sb("wo_c", [P, P])
        s_avg = sb("s_avg", [P, P])
        s_low = sb("s_low", [P, P])
        s_ha = sb("s_ha", [P, P])
        s_hb = sb("s_hb", [P, P])
        bih = sb("bih", [P, 3])
        bhh = sb("bhh", [P, 3])
        brz = sb("brz", [P, 2])
        bi2 = sb("bi2", [P, 1])
        bo_low = sb("bo_low", [P, 1])
        bo_high = sb("bo_high", [P, 1])
        mv = sb("mv", [P, 2, 2])
        sm = sb("sm", [P, 12, 3])
        bseq = sb("bseq", [P, 1])
        zeros = sb("zeros", [P, TILE])
        spare = sb("spare", [P, 48])

        bank = [ctx.enter_context(nc.psum_tensor(f"bank{i}", [P, TILE], fp32)) for i in range(8)]
        rx_ps = [bank[0], bank[3]]
        hn_ps = [bank[1], bank[4]]
        z_ps = [bank[2], bank[5]]
        fin_ps = [bank[0:3], bank[3:6]]
        proj_ps = bank[6:8]
        stat_ps = bank[6]

        w_zeroed = sem("w_zeroed")
        w_loaded = sem("w_loaded")
        w_ready = sem("w_ready")
        x_loaded = [sem(f"x_loaded{i}") for i in range(XSLOTS)]
        x_finished = sem("x_finished")
        out_stored = [sem(f"out_stored{i}") for i in range(XSLOTS)]
        sx_loaded = [sem(f"sx_loaded{i}") for i in range(2)]
        sx_used = [sem(f"sx_used{i}") for i in range(2)]
        stat_dve = sem("stat_dve")
        stat_pe = sem("stat_pe")
        stat_sd = sem("stat_sd")
        proj_ready = sem("proj_ready")
        hi_seq_ready = sem("hi_seq_ready")
        seq_ready = sem("seq_ready")
        hsum_zeroed = sem("hsum_zeroed")
        fin_ready = sem("fin_ready")
        per_step = {name: [sem(f"{name}{c}") for c in range(2)] for name in (
            "pre_r", "pre_n", "pre_z", "r_ready", "z_ready", "t1_ready", "t2_ready",
            "n_ready", "u_ready", "v_ready", "h_ready", "h_added")}
        pre_r, pre_n, pre_z = per_step["pre_r"], per_step["pre_n"], per_step["pre_z"]
        r_ready, z_ready = per_step["r_ready"], per_step["z_ready"]
        t1_ready, t2_ready, n_ready = per_step["t1_ready"], per_step["t2_ready"], per_step["n_ready"]
        u_ready, v_ready = per_step["u_ready"], per_step["v_ready"]
        h_ready, h_added = per_step["h_ready"], per_step["h_added"]
        pro_loaded = [sem(f"pro_loaded{i}") for i in range(PSLOTS)]
        pro_used = [sem(f"pro_used{i}") for i in range(PSLOTS)] 

        NSD = 17
        NSP = 3

        seq_hi_hw = seq_hi[:, :].rearrange("p (h w) -> p h w", w=WW)
        seq_lo_hw = seq_lo[:, :].rearrange("p (h w) -> p h w", w=WW)
        hsum_hw = hsum[:, :].rearrange("p (h w) -> p h w", w=WW)

        def pixels(view, c, back, t):
            s = (T - 1) - t if back else t
            if c == 0:
                return view[:, :, bass.ds(s, 1)].rearrange("p h w -> p (h w)")
            return view[:, bass.ds(s, 1), :].rearrange("p h w -> p (h w)")

        block = ctx.enter_context(nc.Block())

        @block.sync
        def _(sp):
            def load_stats(pair):
                with sp.Fori(0, CPI) as i:
                    for a in range(2):
                        sp.wait_ge(sx_used[a], 1 + CPI * (pair - 1) + i)
                        src = x_flat[bass.ds(2 * pair + a, 1), :, bass.ds(i * CHUNK, CHUNK)]
                        sp.dma_start(sx[:, a, :], src.rearrange("b p m -> (b p) m")).then_inc(sx_loaded[a], 16)

            def load_x(pair, i, s):
                px = bass.ds((i + s) * TILE, TILE)
                images = bass.ds(2 * pair, 2)
                sp.dma_start(xt[:, s, 0:2, :], x_px[images, 0:CLOW, px].rearrange("b c n -> c b n"))\
                  .then_inc(x_loaded[s], 16)
                sp.dma_start(xt[:, s, 2, :], x_px[images, CLOW:C, px])\
                  .then_inc(x_loaded[s], 16)

            def pair_loads(g, stats):
                for s in range(XSLOTS):
                    sp.wait_ge(out_stored[s], 32 * (ROUNDS * g + 1))
                    load_x(g, 0, s)
                with sp.Fori(1, ROUNDS) as j:
                    for s in range(XSLOTS):
                        sp.wait_ge(proj_ready, TILES * g + (j - 1) * XSLOTS + s + 1)
                        load_x(g, j * XSLOTS, s)
                if stats:
                    load_stats(g + 1)
                for s in range(XSLOTS):
                    sp.wait_ge(proj_ready, TILES * g + TILES - XSLOTS + s + 1)
                    load_x(g, 0, s)
                with sp.Fori(1, ROUNDS) as j:
                    for s in range(XSLOTS):
                        sp.wait_ge(out_stored[s], 32 * (ROUNDS * g + j + 1))
                        load_x(g, j * XSLOTS, s)

            with sp.Fori(0, PRO // 2) as j:
                for s in range(PSLOTS):
                    sp.wait_ge(pro_used[s], 1 + j)
                    src = x_flat[s // 2:s // 2 + 1, :, bass.ds((2 * j + s % 2) * 3 * TILE, 3 * TILE)]
                    sp.dma_start(xt[:, s, :, :].rearrange("p k n -> p (k n)"), src.rearrange("b p m -> (b p) m"))\
                      .then_inc(pro_loaded[s], 16)
            for s in range(PSLOTS):
                sp.wait_ge(pro_used[s], 1 + PRO // 2)
            with sp.Fori(0, PAIRS - 1) as g:
                pair_loads(g, True)
            pair_loads(PAIRS - 1, False)

        @block.gpsimd
        def _(pool):
            for weight in (wi_high, wo_a, wo_b, wo_c, wh):
                pool.memset(weight[:], 0.0)
            pool.memset(wx, 0.0).then_inc(w_zeroed, 1)

            def make_v(k, c):
                pool.wait_ge(z_ready[c], k + 2)
                pool.tensor_tensor(v[:, c, :], z[:, c, :], h[:, c, :], ALU.mult).then_inc(v_ready[c], 1)

            def add_h(k, t, c):
                pool.wait_ge(h_ready[c], k + 2)
                pool.wait_ge(h_added[1 - c], k + 1 + c)
                for back in range(2):
                    px = pixels(hsum_hw, c, back, t)
                    ins = pool.tensor_tensor(px, px, h[:, c, back * N:(back + 1) * N], ALU.add)
                ins.then_inc(h_added[c], 1)

            with pool.Fori(0, PAIRS) as g:
                make_v(T * g, 0)
                make_v(T * g, 1)
                pool.wait_ge(hsum_zeroed, TILES * (g + 1))
                add_h(T * g, 0, 0)
                with pool.Fori(1, T) as t:
                    k = T * g + t
                    make_v(k, 0)
                    add_h(k - 1, t - 1, 1)
                    make_v(k, 1)
                    add_h(k, t, 0)
                add_h(T * g + T - 1, T - 1, 1)

        @block.scalar
        def _(act):
            loads = [(wi_low[:, :], wi_t[0:CLOW, :]), (s_avg[:, :], avg_part), (s_low[:, :], sel_low),
                     (s_ha[:, :], sel_high_a), (s_hb[:, :], sel_high_b)]
            bo_col = bo.rearrange("(c o) -> c o", o=1)
            bi_col = bi.rearrange("(c o) -> c o", o=1)
            loads.append((bo_low[:, :], bo_col[0:CLOW, :]))
            act.wait_ge(w_zeroed, 1)
            for k in range(2):
                half = slice(k * D, (k + 1) * D)
                loads += [(wi_high[half, half], wi_t[CLOW:C, :]),
                          (wo_c[half, half], wo_t[:, CLOW:C]),
                          ((wo_a, wo_b)[k][half, :], wo_t[:, 0:CLOW]),
                          (bi2[half, :], bi_col),
                          (bo_high[half, :], bo_col[CLOW:C, :])]
                for g in range(3):
                    loads += [(wx[half, g, half], w_ih_t[:, g * D:(g + 1) * D]),
                              (wh[half, g, half], w_hh_t[:, g * D:(g + 1) * D]),
                              (bih[half, g:g + 1], b_ih.rearrange("(c o) -> c o", o=1)[g * D:(g + 1) * D, :]),
                              (bhh[half, g:g + 1], b_hh.rearrange("(c o) -> c o", o=1)[g * D:(g + 1) * D, :])]
            assert len(loads) == N_WEIGHT_LOADS
            for dst, src in loads:
                act.dma_start(dst, src).then_inc(w_loaded, 16)

            def deviation(g):
                act.wait_ge(stat_dve, NSD * g + 6)
                act.activation(sm[:, 1, :], sm[:, 0, :], ACT.Sqrt).then_inc(stat_sd, 1)
                act.preload_act_table(ACT.Sigmoid)

            def project_and_scan(g):
                act.wait_ge(stat_dve, NSD * g + NSD)
                with act.Fori(0, TILES // 2) as j:
                    for s in range(2):
                        act.wait_ge(proj_ready, TILES * g + 2 * j + s + 1)
                        act.activation(seq_hi[:, bass.ds((2 * j + s) * TILE, TILE)], proj_ps[s][:, :], ACT.Identity,
                                       bias=bseq[:, 0:1]).then_inc(hi_seq_ready, 1)

                with act.Fori(0, T) as t:
                    k = T * g + t
                    for c in range(2):
                        act.wait_ge(pre_r[c], k + 2)
                        act.activation(r[:, c, :], rx_ps[c][:, 0:N2], ACT.Sigmoid, bias=brz[:, 0:1])\
                           .then_inc(r_ready[c], 1)
                        act.wait_ge(pre_z[c], k + 2)
                        act.activation(z[:, c, :], z_ps[c][:, 0:N2], ACT.Sigmoid, bias=brz[:, 1:2])\
                           .then_inc(z_ready[c], 1)
                        act.wait_ge(t2_ready[c], k + 2)
                        act.activation(n[:, c, :], t2[:, c, :], ACT.Tanh, bias=bih[:, 2:3])\
                           .then_inc(n_ready[c], 1)

            def store(g, i, s):
                act.wait_ge(x_finished, XSLOTS + TILES * g + i + 1)
                px = bass.ds(i * TILE, TILE)
                images = bass.ds(2 * g, 2)
                act.dma_start(out_px[images, 0:CLOW, px].rearrange("b c n -> c b n"), xt[:, s, 0:2, :])\
                   .then_inc(out_stored[s], 16)
                act.dma_start(out_px[images, CLOW:C, px], xt[:, s, 2, :])\
                   .then_inc(out_stored[s], 16)

            def finish(g, stats):
                if stats:
                    for s in range(XSLOTS):
                        store(g, s, s)
                        if s == 2:
                            deviation(g + 1)
                with act.Fori(1 if stats else 0, ROUNDS) as j:
                    for s in range(XSLOTS):
                        store(g, j * XSLOTS + s, s)

            deviation(0)
            with act.Fori(0, PAIRS - 1) as g:
                project_and_scan(g)
                finish(g, True)
            project_and_scan(PAIRS - 1)
            finish(PAIRS - 1, False)
            for s in range(XSLOTS):
                act.wait_ge(out_stored[s], 32 * (PAIRS * ROUNDS + 1))

        @block.tensor
        def _(pe):
            pe.wait_ge(w_loaded, 16 * N_WEIGHT_LOADS)

            def group_means(g):
                pe.wait_ge(stat_dve, NSD * g + 2)
                pe.matmul(stat_ps[:, 0:2], s_avg[:, :], mv[:, :, 0], start=True, stop=True).then_inc(stat_pe, 1)

            def channel_stats(g):
                pe.wait_ge(stat_dve, NSD * g + 5)
                pe.matmul(stat_ps[:, 8:10], s_low[:, :], mv[:, 0, :], start=True, stop=True)
                pe.matmul(stat_ps[:, 10:12], s_low[:, :], mv[:, 1, :], start=True, stop=True)
                pe.matmul(stat_ps[:, 12:14], s_ha[:, :], mv[:, 0, :], start=True, stop=False)
                pe.matmul(stat_ps[:, 12:14], s_hb[:, :], mv[:, 1, :], start=False, stop=True).then_inc(stat_pe, 1)

            def mean_bias(g):
                pe.wait_ge(stat_dve, NSD * g + 13)
                pe.matmul(stat_ps[:, 16:17], wi_high[:, :], sm[:, 8, 2:3], start=True, stop=False,
                          skip_group_check=True)
                pe.matmul(stat_ps[0:D, 16:17], wi_low[:, :], sm[:, 8, 0:1], start=False, stop=True,
                          skip_group_check=True)
                pe.matmul(stat_ps[D:P, 16:17], wi_low[:, :], sm[:, 8, 1:2], start=False, stop=True,
                          skip_group_check=True).then_inc(stat_pe, 1)

            def project(g):
                with pe.Fori(0, ROUNDS) as j:
                    i = j * XSLOTS
                    pe.wait_ge(stat_dve, NSD * g + NSD)
                    pe.wait_ge(x_finished, XSLOTS + TILES * g)
                    for s in range(XSLOTS):
                        pe.wait_ge(x_loaded[s], 32 * (2 * ROUNDS * g + j + 1))
                        pe.wait_ge(seq_ready, TILES * g + i + s + 1)
                        ps = proj_ps[s % 2]
                        pe.matmul(ps[:, :], wc[:, :], xt[:, s, 2, :], start=True, stop=False, skip_group_check=True)
                        pe.matmul(ps[0:D, :], wa[:, :], xt[:, s, 0, :], start=False, stop=True,
                                  skip_group_check=True)
                        pe.matmul(ps[D:P, :], wb[:, :], xt[:, s, 1, :], start=False, stop=True,
                                  skip_group_check=True).then_inc(proj_ready, 1)

            def scan(g):
                with pe.Fori(0, T // 2) as j:
                    t0 = j * 2
                    pe.wait_ge(seq_ready, 2 + TILES * (g + 1))
                    for u in range(2):
                        t = t0 + u
                        k = T * g + t
                        for c in range(2):
                            rx, hn, zz = rx_ps[c], hn_ps[c], z_ps[c]

                            def x_part(ps, col, gate, start):
                                products = ((wx_hi, (seq_hi_hw, seq_lo_hw)), (wx_lo, (seq_hi_hw,)))
                                for m, (wt, parts) in enumerate(products):
                                    for view in parts:
                                        for back in range(2):
                                            pe.matmul(ps[:, col + back * N:col + (back + 1) * N], wt[:, gate, :],
                                                      pixels(view, c, back, t), stop=False, skip_group_check=True,
                                                      start=start and m == 0 and view is seq_hi_hw and back == 0)
                            pe.wait_ge(z_ready[c], k + 1)
                            x_part(zz, 0, 1, True)
                            pe.wait_ge(t2_ready[c], k + 1)
                            x_part(rx, 0, 0, True)
                            x_part(rx, N2, 2, False)
                            pe.wait_ge(h_ready[c], k + 1)
                            for ps, gate, ready, start in ((rx, 0, pre_r, False), (hn, 2, pre_n, True),
                                                           (zz, 1, pre_z, False)):
                                pe.matmul(ps[:, 0:N2], wh[:, gate, :], h[:, c, :], start=start, stop=True,
                                          skip_group_check=True).then_inc(ready[c], 1)

            def finish_tile(g, i, s):
                pe.wait_ge(x_finished, XSLOTS - 1 + TILES * g + i)
                hs = hsum[:, bass.ds(i * TILE, TILE)]
                pe.matmul(fin_ps[s][0][:, :], wo_a[:, :], hs, start=True, stop=True)
                pe.matmul(fin_ps[s][1][:, :], wo_b[:, :], hs, start=True, stop=True)
                pe.matmul(fin_ps[s][2][:, :], wo_c[:, :], hs, start=True, stop=True).then_inc(fin_ready, 1)

            def finish(g, stats):
                for c in range(2):
                    pe.wait_ge(h_added[c], 1 + T * (g + 1))
                if stats:
                    finish_tile(g, 0, 0)
                    finish_tile(g, 1, 1)
                    group_means(g + 1)
                    finish_tile(g, 2, 0)
                    channel_stats(g + 1)
                    for i in range(3, 6):
                        finish_tile(g, i, i % 2)
                    mean_bias(g + 1)
                with pe.Fori(3 if stats else 0, TILES // 2) as j:
                    for s in range(2):
                        finish_tile(g, 2 * j + s, s)

            group_means(0)
            channel_stats(0)
            mean_bias(0)
            pe.wait_ge(w_ready, 7)
            with pe.Fori(0, PAIRS - 1) as g:
                project(g)
                scan(g)
                finish(g, True)
            project(PAIRS - 1)
            scan(PAIRS - 1)
            finish(PAIRS - 1, False)

        @block.vector
        def _(dve):
            tokens = [(x_finished, XSLOTS), (seq_ready, 2), (fin_ready, 1)] + [(o, 32) for o in out_stored]
            for c in range(2):
                tokens += [(s, 1) for s in [sx_used[c]] + [chains[c] for chains in per_step.values()]]
            tokens += [(s, 1) for s in pro_used]
            for k, (token, count) in enumerate(tokens):
                dve.memset(spare[:, k:k + 1], 0.0).then_inc(token, count)
            dve.memset(zeros[:, :], 0.0).then_inc(w_ready, 1)

            def weights_prepared():
                dve.wait_ge(w_loaded, 16 * N_WEIGHT_LOADS)
                dve.tensor_tensor(brz[:, 0:2], bih[:, 0:2], bhh[:, 0:2], ALU.add).then_inc(w_ready, 1)
                dve.tensor_scalar(wo_a[:, :], wo_a[:, :], 0.25, None, ALU.mult).then_inc(w_ready, 1)
                dve.tensor_scalar(wo_b[:, :], wo_b[:, :], 0.25, None, ALU.mult).then_inc(w_ready, 1)
                dve.tensor_scalar(wo_c[:, :], wo_c[:, :], 0.25, None, ALU.mult).then_inc(w_ready, 1)
                dve.tensor_copy(wx_hi[:, :, :], wx).then_inc(w_ready, 1)
                dve.wait_ge(w_ready, 6)
                dve.tensor_tensor(wx_lo[:, :, :], wx, wx_hi[:, :, :], ALU.subtract).then_inc(w_ready, 1)

            def chunk_stats(pair, i, a, k):
                if k == 0:
                    dve.wait_ge(sx_loaded[a], 16 * (CPI * (pair - 1) + i + 1))
                ins = dve.bn_stats(bn[:, a, :].rearrange("p (s k) -> p s k", k=12)[:, bass.ds(i, 1), 6 * k:6 * k + 6]
                                   .rearrange("p s k -> p (s k)"), sx[:, a, k * BNF:(k + 1) * BNF])
                if k == 1:
                    ins.then_inc(sx_used[a], 1)

            def scan(g, stats):
                def step(i, u):
                    k = T * g + UN * i + u
                    for c in range(2):
                        dve.wait_ge(r_ready[c], k + 2)
                        dve.wait_ge(pre_n[c], k + 2)
                        dve.scalar_tensor_tensor(out=t1[:, c, :], in0=hn_ps[c][:, 0:N2], scalar=bhh[:, 2:3],
                                                 in1=r[:, c, :], op0=ALU.add, op1=ALU.mult).then_inc(t1_ready[c], 1)
                        dve.wait_ge(t1_ready[c], k + 2)
                        dve.tensor_tensor(t2[:, c, :], rx_ps[c][:, N2:2 * N2], t1[:, c, :], ALU.add)\
                           .then_inc(t2_ready[c], 1)
                        if stats and u % 2 == c:
                            chunk_stats(g + 1, i, u // 2, u % 2)
                        dve.wait_ge(n_ready[c], k + 2)
                        dve.scalar_tensor_tensor(out=u_n[:, c, :], in0=z[:, c, :], scalar=1.0, in1=n[:, c, :],
                                                 op0=ALU.subtract, op1=ALU.mult).then_inc(u_ready[c], 1)
                        dve.wait_ge(u_ready[c], k + 2)
                        dve.wait_ge(v_ready[c], k + 2)
                        dve.tensor_tensor(h[:, c, :], v[:, c, :], u_n[:, c, :], ALU.subtract).then_inc(h_ready[c], 1)

                with dve.Fori(0, T // UN) as i:
                    for u in range(UN):
                        step(i, u)

            def stat_done(g, k):
                dve.wait_ge(stat_dve, NSD * g + k)

            def stats_of_groups(g):
                for c in range(2):
                    dve.wait_ge(h_added[c], 1 + T * g)
                    dve.wait_ge(sx_used[c], 1 + CPI * g)
                    dve.memset(h[:, c, :], 0.0)
                for a in range(2):
                    dve.bn_aggr(mv[:, a, :], bn[:, a, :]).then_inc(stat_dve, 1)

            def mean_squares(g):
                stat_done(g, 2)
                dve.wait_ge(stat_pe, NSP * g + 1)
                dve.tensor_tensor(sm[:, 2, 0:2], mv[:, :, 0], stat_ps[:, 0:2], ALU.subtract).then_inc(stat_dve, 1)
                stat_done(g, 3)
                dve.tensor_tensor(sm[:, 3, 0:2], sm[:, 2, 0:2], sm[:, 2, 0:2], ALU.mult).then_inc(stat_dve, 1)
                stat_done(g, 4)
                dve.tensor_tensor(mv[:, :, 1], mv[:, :, 1], sm[:, 3, 0:2], ALU.add).then_inc(stat_dve, 1)

            def channel_variance(g):
                dve.wait_ge(stat_pe, NSP * g + 2)
                chan = stat_ps[:, 8:14].rearrange("p (i k) -> p i k", k=2)
                dve.tensor_scalar(sm[:, 0, :], chan[:, :, 1], EPS, None, ALU.add).then_inc(stat_dve, 1)
                dve.tensor_copy(sm[:, 4, :], chan[:, :, 0]).then_inc(stat_dve, 1)

            def scaled_weights(g):
                dve.wait_ge(stat_sd, g + 1)
                dve.reciprocal(sm[:, 5, :], sm[:, 1, :]).then_inc(stat_dve, 1)
                stat_done(g, 8)
                dve.tensor_tensor(sm[:, 6, :], sm[:, 5, :], sm[:, 5, :], ALU.mult).then_inc(stat_dve, 1)
                stat_done(g, 9)
                dve.tensor_tensor(sm[:, 7, :], sm[:, 6, :], sm[:, 0, :], ALU.mult).then_inc(stat_dve, 1)
                stat_done(g, 10)
                dve.tensor_scalar(sm[:, 10, :], sm[:, 7, :], -0.5, 1.5, ALU.mult, ALU.add).then_inc(stat_dve, 1)
                stat_done(g, 11)
                dve.tensor_tensor(sm[:, 11, :], sm[:, 5, :], sm[:, 10, :], ALU.mult).then_inc(stat_dve, 1)
                stat_done(g, 12)
                dve.scalar_tensor_tensor(out=sm[:, 8, :], in0=sm[:, 4, :], scalar=-1.0, in1=sm[:, 11, :],
                                         op0=ALU.mult, op1=ALU.mult).then_inc(stat_dve, 1)
                dve.tensor_scalar(wa[:, :], wi_low[:, :], sm[:, 11, 0:1], None, ALU.mult).then_inc(stat_dve, 1)
                dve.tensor_scalar(wb[:, :], wi_low[:, :], sm[:, 11, 1:2], None, ALU.mult).then_inc(stat_dve, 1)
                dve.tensor_scalar(wc[:, :], wi_high[:, :], sm[:, 11, 2:3], None, ALU.mult).then_inc(stat_dve, 1)

            def seq_bias(g):
                dve.wait_ge(stat_pe, NSP * g + 3)
                dve.tensor_tensor(bseq[:, :], stat_ps[:, 16:17], bi2[:, :], ALU.add).then_inc(stat_dve, 1)

            def project(g):
                with dve.Fori(0, TILES // 2) as j:
                    for s in range(2):
                        dve.wait_ge(hi_seq_ready, TILES * g + 2 * j + s + 1)
                        px = bass.ds((2 * j + s) * TILE, TILE)
                        dve.scalar_tensor_tensor(out=seq_lo[:, px], in0=proj_ps[s][:, :], scalar=bseq[:, 0:1],
                                                 in1=seq_hi[:, px], op0=ALU.add, op1=ALU.subtract)\
                           .then_inc(seq_ready, 1)
                        dve.wait_ge(fin_ready, 1 + TILES * g)
                        dve.tensor_copy(hsum[:, px], zeros[:, :]).then_inc(hsum_zeroed, 1)

            def finish_tile(g, j, s):
                dve.wait_ge(fin_ready, 1 + TILES * g + j * XSLOTS + s + 1)
                dve.wait_ge(x_loaded[s], 32 * ((2 * g + 1) * ROUNDS + j + 1))
                for k in range(3):
                    ins = dve.scalar_tensor_tensor(
                        out=xt[:, s, k, :], in0=fin_ps[s % 2][k][:, :],
                        scalar=(bo_low if k < 2 else bo_high)[:, 0:1], in1=xt[:, s, k, :],
                        op0=ALU.add, op1=ALU.add)
                ins.then_inc(x_finished, 1)

            def finish(g, stats):
                if stats:
                    parts = {0: stats_of_groups, 1: mean_squares, 2: channel_variance, 3: scaled_weights}
                    for s in range(XSLOTS):
                        finish_tile(g, 0, s)
                        if s in parts:
                            parts[s](g + 1)
                with dve.Fori(1 if stats else 0, ROUNDS) as j:
                    for s in range(XSLOTS):
                        finish_tile(g, j, s)
                if stats:
                    seq_bias(g + 1)

            with dve.Fori(0, PRO // 2) as j:
                for s in range(PSLOTS):
                    dve.wait_ge(pro_loaded[s], 16 * (j + 1))
                    flat = xt[:, s, :, :].rearrange("p k n -> p (k n)")
                    per = 3 * TILE // BNF
                    for k in range(per):
                        ins = dve.bn_stats(bn[:, s // 2, bass.ds((2 * j + s % 2) * 6 * per + 6 * k, 6)],
                                           flat[:, k * BNF:(k + 1) * BNF])
                    ins.then_inc(pro_used[s], 1)
            for s in range(PSLOTS):
                dve.wait_ge(pro_used[s], 1 + PRO // 2)
            for part in (stats_of_groups, mean_squares, channel_variance):
                part(0)
            weights_prepared()
            scaled_weights(0)
            seq_bias(0)
            with dve.Fori(0, PAIRS - 1) as g:
                project(g)
                scan(g, True)
                finish(g, True)
            project(PAIRS - 1)
            scan(PAIRS - 1, False)
            finish(PAIRS - 1, False)


def kernel(x, L0_conv_Wi, L0_conv_bi, L0_conv_W_ih, L0_conv_W_hh, L0_conv_b_ih, L0_conv_b_hh, L0_conv_Wo, L0_conv_bo):
    import numpy as np
    import concourse.bacc as bacc
    from concourse.bass_utils import run_bass_kernel_spmd

    part = np.arange(128) // 4
    chan = np.arange(192) // 6
    share = np.float32(0.25)
    avg_part = (part[:, None] == part[None, :]).astype(np.float32) * share
    sel = (part[:, None] == chan[None, :]).astype(np.float32) * share
    sel_high_a = np.zeros((128, 128), np.float32)
    sel_high_b = np.zeros((128, 128), np.float32)
    sel_high_a[:, 0:64] = sel[:, 128:192]
    sel_high_b[:, 64:128] = sel[:, 128:192]

    arrays = {
        "x": np.ascontiguousarray(x),
        "wi_t": np.ascontiguousarray(np.asarray(L0_conv_Wi).T),
        "bi": np.ascontiguousarray(L0_conv_bi),
        "w_ih_t": np.ascontiguousarray(np.asarray(L0_conv_W_ih).T),
        "w_hh_t": np.ascontiguousarray(np.asarray(L0_conv_W_hh).T),
        "b_ih": np.ascontiguousarray(L0_conv_b_ih),
        "b_hh": np.ascontiguousarray(L0_conv_b_hh),
        "wo_t": np.ascontiguousarray(np.asarray(L0_conv_Wo).T),
        "bo": np.ascontiguousarray(L0_conv_bo),
        "avg_part": avg_part,
        "sel_low": np.ascontiguousarray(sel[:, 0:128]),
        "sel_high_a": sel_high_a,
        "sel_high_b": sel_high_b,
    }
    nc = bacc.Bacc("TRN2", target_bir_lowering=False, num_devices=1)
    args = [nc.dram_tensor(name, a.shape, mybir.dt.from_np(a.dtype), kind="ExternalInput").ap()
            for name, a in arrays.items()]
    out = nc.dram_tensor("out", arrays["x"].shape, mybir.dt.float32, kind="ExternalOutput").ap()
    gru_scan_2d_kernel(nc, *args, out)
    return run_bass_kernel_spmd(nc, [arrays], core_ids=[0]).results[0]["out"]
```
